# Optimizing a Trainium2 kernel written in Bass

```python
import numpy as np
import jax
import jax.numpy as jnp

def _softmax(x, axis=-1):
    return jax.nn.softmax(x, axis=axis)

def _gelu(x):
    return jax.nn.gelu(x, approximate=True)

def _silu(x):
    return jax.nn.silu(x)

def _sigmoid(x):
    return jax.nn.sigmoid(x)

def _layernorm(x, axis=-1, eps=1e-05):
    m = jnp.mean(x, axis=axis, keepdims=True)
    v = jnp.var(x, axis=axis, keepdims=True)
    return (x - m) / jnp.sqrt(v + eps)

def _scatter_add(tgt, idx, src, axis=0):
    return tgt.at[idx].add(src)

def _segment_sum(src, seg, n):
    return jax.ops.segment_sum(src, seg, n)
kernel_name = 'mk_flamingo_gated_d1_seqx_r2_aa9eff'

def setup_inputs(seed: int=0):
    np.random.seed(seed)
    _w = jnp.asarray

    def _rec_inputs():
        import jax
        import jax.numpy as jnp
        _rk = jax.random.key(seed)
        x = -0.0002928 + 1 * jax.random.normal(jax.random.fold_in(_rk, 1), (4, 1024, 512), jnp.float32)
        _lenS = 1024 - jax.random.randint(jax.random.fold_in(_rk, 7), (4,), 0, max(1, 1024 // 4) + 1, jnp.int32)
        _lenS2 = 1024 - jax.random.randint(jax.random.fold_in(_rk, 8), (4,), 0, max(1, 1024 // 4) + 1, jnp.int32)
        _ctx_1024P = jax.random.normal(jax.random.fold_in(_rk, 11), (4, 16, 512), jnp.float32)
        _ctx_1024c = jax.random.dirichlet(jax.random.fold_in(_rk, 511), 0.3 * jnp.ones((16,), jnp.float32), (4, 1024))
        _ctx_1024t = jnp.einsum('bsk,bkd->bsd', _ctx_1024c, _ctx_1024P)
        _ctx_1024t = _ctx_1024t * jax.lax.rsqrt(jnp.mean(jnp.square(_ctx_1024t)) + 1e-12) * 0.953939
        ctx_1024 = -1.39393e-06 + 0.999914 * (_ctx_1024t + 0.3 * jax.random.normal(jax.random.fold_in(_rk, 611), (4, 1024, 512), jnp.float32))
        _g = jax.random.normal(jax.random.fold_in(_rk, 9001), (2, 1), jnp.float32)
        _g = jnp.sign(_g) * jnp.maximum(jnp.abs(_g), 1.0) + (_g == 0) * 1.0
        g_xattn = _g[0]
        g_ffn = _g[1]
        return (x, ctx_1024, g_xattn, g_ffn)
    x, ctx_1024, g_xattn, g_ffn = _rec_inputs()

    def _L0_xattn_setup():
        import jax, jax.numpy as jnp
        import numpy as np
        N_EMBD = 512
        N_HEAD = 16
        DIM_HEAD = N_EMBD // N_HEAD
        SCALE = DIM_HEAD ** (-0.5)
        key = jax.random.key(seed)
        ks = jax.random.split(key, 6)
        B, Tq, Tkv = (2, 1024, 1024)
        x_q = jax.random.normal(ks[0], (B, Tq, N_EMBD), dtype=jnp.float32)
        x_kv = jax.random.normal(ks[1], (B, Tkv, N_EMBD), dtype=jnp.float32)
        position_bias = jax.random.normal(ks[2], (1, N_HEAD, Tq, Tkv), dtype=jnp.float32)
        s = 0.02
        W_q = jax.random.normal(ks[3], (N_EMBD, N_EMBD), dtype=jnp.float32) * s
        W_kv = jax.random.normal(ks[4], (N_EMBD, 2 * N_EMBD), dtype=jnp.float32) * s
        W_proj = jax.random.normal(ks[5], (N_EMBD, N_EMBD), dtype=jnp.float32) * s
        return {'x_q': x_q, 'x_kv': x_kv, 'position_bias': position_bias, 'W_q': W_q, 'W_kv': W_kv, 'W_proj': W_proj}
    _L0_xattn_all = _L0_xattn_setup()
    _L0_xattn_in = {k: v for k, v in _L0_xattn_all.items() if k in ('position_bias', 'W_q', 'W_kv', 'W_proj')}
    del _L0_xattn_all

    def _L0_ffn_setup():
        import jax, jax.numpy as jnp
        import numpy as np
        D_MODEL = 512
        D_FF = 2048
        NUM_EXPERTS = 8
        B, N = (16, 512)
        key = jax.random.key(seed)
        ks = jax.random.split(key, 7)
        s_in = 1.0 / np.sqrt(D_MODEL)
        s_ff = 1.0 / np.sqrt(D_FF)
        return {'x': jax.random.normal(ks[0], (B, N, D_MODEL), dtype=jnp.float32), 'Wr': jax.random.uniform(ks[1], (D_MODEL, NUM_EXPERTS), jnp.float32, -s_in, s_in), 'br': jax.random.uniform(ks[2], (NUM_EXPERTS,), jnp.float32, -s_in, s_in), 'W1': jax.random.uniform(ks[3], (NUM_EXPERTS, D_MODEL, D_FF), jnp.float32, -s_in, s_in), 'b1': jax.random.uniform(ks[4], (NUM_EXPERTS, D_FF), jnp.float32, -s_in, s_in), 'W2': jax.random.uniform(ks[5], (NUM_EXPERTS, D_FF, D_MODEL), jnp.float32, -s_ff, s_ff), 'b2': jax.random.uniform(ks[6], (NUM_EXPERTS, D_MODEL), jnp.float32, -s_ff, s_ff)}
    _L0_ffn_all = _L0_ffn_setup()
    _L0_ffn_in = {k: v for k, v in _L0_ffn_all.items() if k in ('Wr', 'br', 'W1', 'b1', 'W2', 'b2')}
    del _L0_ffn_all
    return {'x': x, 'ctx_1024': ctx_1024, 'g_xattn': g_xattn, 'g_ffn': g_ffn, 'L0_xattn_position_bias': _L0_xattn_in['position_bias'], 'L0_xattn_W_q': _L0_xattn_in['W_q'], 'L0_xattn_W_kv': _L0_xattn_in['W_kv'], 'L0_xattn_W_proj': _L0_xattn_in['W_proj'], 'L0_ffn_Wr': _L0_ffn_in['Wr'], 'L0_ffn_br': _L0_ffn_in['br'], 'L0_ffn_W1': _L0_ffn_in['W1'], 'L0_ffn_b1': _L0_ffn_in['b1'], 'L0_ffn_W2': _L0_ffn_in['W2'], 'L0_ffn_b2': _L0_ffn_in['b2']}

def reference(x, ctx_1024, g_xattn, g_ffn, L0_xattn_position_bias, L0_xattn_W_q, L0_xattn_W_kv, L0_xattn_W_proj, L0_ffn_Wr, L0_ffn_br, L0_ffn_W1, L0_ffn_b1, L0_ffn_W2, L0_ffn_b2):
    import jax
    import jax.numpy as jnp

    def _L0_xattn_ref(x_q, x_kv, position_bias, W_q, W_kv, W_proj):
        import jax, jax.numpy as jnp
        import numpy as np
        N_EMBD = 512
        N_HEAD = 16
        DIM_HEAD = N_EMBD // N_HEAD
        SCALE = DIM_HEAD ** (-0.5)
        B, Tq, C = x_q.shape
        Tkv = x_kv.shape[1]
        q = x_q @ W_q
        kv = x_kv @ W_kv
        k, v = (kv[..., :C], kv[..., C:])
        q = q.reshape(B, Tq, N_HEAD, DIM_HEAD).transpose(0, 2, 1, 3)
        k = k.reshape(B, Tkv, N_HEAD, DIM_HEAD).transpose(0, 2, 1, 3)
        v = v.reshape(B, Tkv, N_HEAD, DIM_HEAD).transpose(0, 2, 1, 3)
        attn = jnp.einsum('bhqd,bhkd->bhqk', q, k)
        attn = attn + position_bias
        attn = attn / SCALE
        attn = jax.nn.softmax(attn, axis=-1)
        y = jnp.einsum('bhqk,bhkd->bhqd', attn, v)
        y = y.transpose(0, 2, 1, 3).reshape(B, Tq, C)
        return y @ W_proj

    def _L0_ffn_ref(x, Wr, br, W1, b1, W2, b2):
        import jax, jax.numpy as jnp
        import numpy as np
        D_MODEL = 512
        D_FF = 2048
        NUM_EXPERTS = 8
        B, N = (16, 512)
        scores = jnp.einsum('bh,he->be', x.mean(axis=1), Wr) + br
        top1 = jnp.argmax(scores, axis=-1)
        w1 = W1[top1]
        c1 = b1[top1]
        w2 = W2[top1]
        c2 = b2[top1]
        h = jax.nn.relu(jnp.einsum('bnh,bhf->bnf', x, w1) + c1[:, None, :])
        out = jnp.einsum('bnf,bfh->bnh', h, w2) + c2[:, None, :]
        return out
    x = x + jnp.tanh(g_xattn[0]) * _L0_xattn_ref(_layernorm(x, axis=-1), ctx_1024, L0_xattn_position_bias, L0_xattn_W_q, L0_xattn_W_kv, L0_xattn_W_proj)
    x = x + jnp.tanh(g_ffn[0]) * _L0_ffn_ref(_layernorm(x, axis=-1), L0_ffn_Wr, L0_ffn_br, L0_ffn_W1, L0_ffn_b1, L0_ffn_W2, L0_ffn_b2)
    return x

_drawn_inputs = setup_inputs


def setup_inputs(seed=0):
    import zlib

    import numpy as np

    out = dict(_drawn_inputs(seed))
    spreads = {}
    factors = {'L0_ffn_b1': 6.012, 'L0_ffn_b2': 4.819}
    for name, (base, spread) in spreads.items():
        noise = np.random.default_rng([zlib.crc32(name.encode()), seed]).standard_normal(out[name].shape)
        drawn = base * np.exp(spread * noise) if base else spread * noise
        out[name] = jnp.asarray(drawn.astype(out[name].dtype))
    for name, factor in factors.items():
        out[name] = (out[name] * factor).astype(out[name].dtype)
    return out
```

```python
import concourse.bass as bass
from concourse import mybir
from contextlib import ExitStack

F32 = mybir.dt.float32
F32R = mybir.dt.float32r
U32 = mybir.dt.uint32
ALU = mybir.AluOpType
ACT = mybir.ActivationFunctionType
AX = mybir.AxisListType

P = 128
TB = 512
TT = TB // P
EPS = 1e-5


def wait_count(eng, sem, n):
    if not (isinstance(n, int) and n <= 0):
        eng.wait_ge(sem, n)


def wait_apart(eng, sem, n):
    if isinstance(n, int):
        eng.wait_ge(sem, n)
    else:
        count = eng.to_reg(n)
        eng.wait_ge(sem, 1)
        eng.wait_ge(sem, count)


def repeat(eng, n, body):
    body(0)
    with eng.Fori(1, n - 1) as i:
        body(i)
    body(n - 1)


def is_last(i, n):
    return isinstance(i, int) and i == n - 1


def raw(ap):
    return ap.bitcast(F32)


def gated_block(nc, x, ctxT, g_xattn, g_ffn, bias, Wq, Wkv, Wproj, Wr, br, W1c, b1c, W2, b2, out):
    B, T, D = x.shape
    H = bias.shape[1]
    DH = D // H
    S = ctxT.shape[2]
    NE, NF, _, CTF = W1c.shape
    CT = D // P
    HB = T // TB
    NQ = T // P
    NKT = S // P
    INV_SCALE = float(DH) ** 0.5
    assert (D, DH, T, S, HB, CTF) == (CT * P, 32, NQ * P, T, 2, CT * P)

    q_scr = nc.dram_tensor("q_scr", (B, D, 2, T), F32, kind="Internal").ap()
    k_scr = nc.dram_tensor("k_scr", (B, D, 2, S), F32, kind="Internal").ap()
    v_scr = nc.dram_tensor("v_scr", (B, H, P, NKT * DH), F32, kind="Internal").ap()
    o_scr = nc.dram_tensor("o_scr", (H, DH + 1, B * T), F32, kind="Internal").ap()
    r_scr = nc.dram_tensor("r_scr", (H, B * T), F32, kind="Internal").ap()
    x1_scr = nc.dram_tensor("x1_scr", (B * T, D), F32, kind="Internal").ap()
    z2_scr = nc.dram_tensor("z2_scr", (B * HB, P, 2, CT, TB), F32, kind="Internal").ap()

    with ExitStack() as top:
        ident = top.enter_context(nc.sbuf_tensor("ident", [P, P], F32))
        experts = top.enter_context(nc.sbuf_tensor("experts", [1, B, 8], U32))
        project_qkv(nc, x, ctxT, Wq, Wkv, q_scr, k_scr, v_scr, ident)
        attention(nc, bias, q_scr, k_scr, v_scr, o_scr, ident, B, T, S, H, DH, INV_SCALE)
        project_out(nc, x, g_xattn, Wproj, Wr, br, o_scr, r_scr, x1_scr, z2_scr, ident, experts)
        expert_ffn(nc, g_ffn, W1c, b1c, W2, b2, x1_scr, z2_scr, experts, out, B, T)


def project_qkv(nc, x, ctxT, Wq, Wkv, q_scr, k_scr, v_scr, ident):
    B, T, D = x.shape
    CT, HB, DH = D // P, T // TB, 32
    H = D // DH
    OUTS = 3 * CT
    with ExitStack() as c:
        def sb(name, shape, dt=F32):
            return c.enter_context(nc.sbuf_tensor(name, shape, dt))

        def sem(name):
            return c.enter_context(nc.semaphore(name))

        wq_raw = sb("wq_raw", [P, CT, D])
        wkv_raw = sb("wkv_raw", [P, CT, 2 * D])
        wq_hi, wq_lo = sb("wq_hi", [P, CT, D], F32R), sb("wq_lo", [P, CT, D], F32R)
        wkv_hi, wkv_lo = sb("wkv_hi", [P, CT, 2 * D], F32R), sb("wkv_lo", [P, CT, 2 * D], F32R)
        xin = sb("xin", [P, HB, TT, D])
        cin = sb("cin", [P, HB, CT, TB])
        c_hi, c_lo = sb("c_hi", [P, CT, TB], F32R), sb("c_lo", [P, CT, TB], F32R)
        z = sb("z", [P, TT, D])
        z_hi, z_lo = sb("z_hi", [P, CT, TB], F32R), sb("z_lo", [P, CT, TB], F32R)
        qk_out = sb("qk_out", [P, 4, 2, TB], F32R)
        v_out = sb("v_out", [P, H, DH, HB * TT])
        stats = sb("stats", [P, TT, 6])
        moments = sb("moments", [P, TT, 2])
        var_eps = sb("var_eps", [P, TT])
        rstd = sb("rstd", [P, TT])
        minus_half = sb("minus_half", [P, TT])
        zT_ps = c.enter_context(nc.psum_tensor("zT_ps", [P, 2, TB], F32))
        out_ps = c.enter_context(nc.psum_tensor("out_ps", [P, 4, TB], F32))

        wkv_loaded, wq_loaded = sem("wkv_loaded"), sem("wq_loaded")
        x_loaded = [sem(f"x_loaded{u}") for u in range(HB)]
        c_loaded = [sem(f"c_loaded{u}") for u in range(HB)]
        w_hi_ready, w_lo_ready = sem("w_hi_ready"), sem("w_lo_ready")
        ident_ready, const_ready = sem("ident_ready"), sem("const_ready")
        c_hi_ready, c_lo_ready = sem("c_hi_ready"), sem("c_lo_ready")
        stats_ready, moments_ready, rstd_ready = sem("stats_ready"), sem("moments_ready"), sem("rstd_ready")
        eps_added = sem("eps_added")
        z_ready, zT_ready, z_hi_ready, z_lo_ready = sem("z_ready"), sem("zT_ready"), sem("z_hi_ready"), sem("z_lo_ready")
        out_ready = sem("out_ready")
        act_out, dve_out = sem("act_out"), sem("dve_out")
        qk_stored = [sem(f"qk_stored{i}") for i in range(4)]
        v_stored = sem("v_stored")

        block = c.enter_context(nc.Block())

        @block.sync
        def _(sp):
            sp.dma_start(wkv_raw[:, :, :], Wkv.rearrange("(c p) n -> p c n", p=P)).then_inc(wkv_loaded, 16)

            def loads(b):
                for u in range(HB):
                    t = HB * b + u
                    wait_count(sp, c_lo_ready, t - 1)
                    sp.dma_start(cin[:, u, :, :], ctxT[b, :, u * TB:(u + 1) * TB].rearrange("(c p) t -> p c t", p=P)
                                 ).then_inc(c_loaded[u], 16)
                    wait_count(sp, z_ready, t - 1)
                    sp.dma_start(xin[:, u, :, :], x[b, u * TB:(u + 1) * TB, :].rearrange("(j p) n -> p j n", p=P)
                                 ).then_inc(x_loaded[u], 16)
                    if isinstance(b, int) and t == 0:
                        sp.dma_start(wq_raw[:, :, :], Wq.rearrange("(c p) n -> p c n", p=P)).then_inc(wq_loaded, 16)

            repeat(sp, B, loads)

        @block.gpsimd
        def _(pool):
            pool.memset(ident[:, :], 0.0).then_inc(ident_ready, 1)
            pool.memset(minus_half[:, :], -0.5).then_inc(const_ready, 1)
            pool.wait_ge(ident_ready, 1)
            pool.affine_select(out=ident[:, :], in_=ident[:, :], compare_op=ALU.not_equal, fill=1.0,
                               base=0, pattern=[[-1, P]], channel_multiplier=1).then_inc(ident_ready, 1)
            pool.wait_ge(const_ready, 1)

            def body(b):
                for u in range(HB):
                    t = HB * b + u
                    pool.wait_ge(c_hi_ready, t + 1)
                    pool.tensor_tensor(c_lo[:, :, :], cin[:, u, :, :], raw(c_hi[:, :, :]), ALU.subtract
                                       ).then_inc(c_lo_ready, 1)
                    pool.wait_ge(eps_added, t + 1)
                    wait_count(pool, z_ready, t)
                    pool.tensor_tensor(rstd[:, :], var_eps[:, :], minus_half[:, :], ALU.pow).then_inc(rstd_ready, 1)

            repeat(pool, B, body)

        @block.scalar
        def _(act):
            def take_hi(t, i, s):
                slot = s % 4
                wait_count(act, qk_stored[slot], 16 * (2 * t + s // 4))
                act.wait_ge(out_ready, OUTS * t + i + 1)
                act.activation(qk_out[:, slot, 0, :], out_ps[:, i % 4, :], ACT.Copy).then_inc(act_out, 1)

            def store(scr, t, b, u, ct, s):
                slot = s % 4
                act.wait_ge(dve_out, 2 * CT * t + s + 1)
                act.dma_start(scr[b, ct * P:(ct + 1) * P, :, u * TB:(u + 1) * TB], raw(qk_out[:, slot, :, :])
                              ).then_inc(qk_stored[slot], 16)

            def body(b):
                for u in range(HB):
                    t = HB * b + u
                    for i in range(CT):
                        take_hi(t, i, i)
                        if i:
                            store(k_scr, t, b, u, i - 1, i - 1)
                    for ct in range(CT):
                        act.wait_ge(zT_ready, CT * t + ct + 1)
                        act.activation(z_hi[:, ct, :], zT_ps[:, ct % 2, :], ACT.Copy).then_inc(z_hi_ready, 1)
                        if ct == 0:
                            store(k_scr, t, b, u, CT - 1, CT - 1)
                    wait_count(act, v_stored, 16 * b)
                    for j in range(TT):
                        i = CT + j
                        act.wait_ge(out_ready, OUTS * t + i + 1)
                        act.activation(v_out[:, :, :, u * TT + j], out_ps[:, i % 4, :].rearrange("p (h d) -> p h d", h=H),
                                       ACT.Copy).then_inc(act_out, 1)
                    if u == HB - 1:
                        act.wait_ge(act_out, OUTS * t + 2 * CT)
                        act.dma_start(v_scr[b, :, :, :].rearrange("h p n -> p h n"),
                                      v_out[:, :, :, :].rearrange("p h d j -> p h (d j)")).then_inc(v_stored, 16)
                    for ct in range(CT):
                        take_hi(t, 2 * CT + ct, CT + ct)
                        if ct:
                            store(q_scr, t, b, u, ct - 1, CT + ct - 1)
                    store(q_scr, t, b, u, CT - 1, 2 * CT - 1)

            repeat(act, B, body)
            for i in range(4):
                act.wait_ge(qk_stored[i], 16 * 2 * B * HB)
            act.wait_ge(v_stored, 16 * B)

        @block.vector
        def _(dve):
            def split_weight(hi, lo, w):
                n = split_weight.n = split_weight.n + 1
                dve.tensor_copy(hi, w).then_inc(w_hi_ready, 1)
                dve.wait_ge(w_hi_ready, n)
                dve.tensor_tensor(lo, w, raw(hi), ALU.subtract).then_inc(w_lo_ready, 1)
            split_weight.n = 0

            def prepare_ctx(t, u, b):
                dve.wait_ge(c_loaded[u], 16 * (b + 1))
                wait_count(dve, out_ready, OUTS * t - CT)
                dve.tensor_copy(c_hi[:, :, :], cin[:, u, :, :]).then_inc(c_hi_ready, 1)

            def prepare_x(t, u, b):
                dve.wait_ge(x_loaded[u], 16 * (b + 1))
                for j in range(TT):
                    last = dve.bn_stats(stats[:, j, :], xin[:, u, j, :])
                last.then_inc(stats_ready, 1)
                wait_apart(dve, stats_ready, t + 1)
                for j in range(TT):
                    last = dve.bn_aggr(moments[:, j, :], stats[:, j, :])
                last.then_inc(moments_ready, 1)
                dve.wait_ge(moments_ready, t + 1)
                wait_count(dve, rstd_ready, t)
                dve.tensor_scalar(var_eps[:, :], moments[:, :, 1], EPS, None, ALU.add).then_inc(eps_added, 1)
                dve.wait_ge(rstd_ready, t + 1)
                wait_count(dve, zT_ready, CT * t)
                for j in range(TT):
                    last = dve.tensor_scalar(z[:, j, :], xin[:, u, j, :], moments[:, j, 0:1], rstd[:, j:j + 1],
                                             ALU.subtract, ALU.mult)
                last.then_inc(z_ready, 1)

            def take_lo(t, i, s):
                dve.wait_ge(act_out, OUTS * t + i + 1)
                dve.tensor_tensor(qk_out[:, s % 4, 1, :], out_ps[:, i % 4, :], raw(qk_out[:, s % 4, 0, :]),
                                  ALU.subtract).then_inc(dve_out, 1)

            dve.wait_ge(wkv_loaded, 16)
            split_weight(wkv_hi[:, :, 0:D], wkv_lo[:, :, 0:D], wkv_raw[:, :, 0:D])
            prepare_ctx(0, 0, 0)
            split_weight(wkv_hi[:, :, D:2 * D], wkv_lo[:, :, D:2 * D], wkv_raw[:, :, D:2 * D])
            prepare_x(0, 0, 0)
            dve.wait_ge(wq_loaded, 16)
            split_weight(wq_hi[:, :, :], wq_lo[:, :, :], wq_raw[:, :, :])

            def body(b):
                for u in range(HB):
                    t = HB * b + u
                    for i in range(CT):
                        take_lo(t, i, i)
                    for ct in range(CT):
                        dve.wait_ge(z_hi_ready, CT * t + ct + 1)
                        dve.tensor_tensor(z_lo[:, ct, :], zT_ps[:, ct % 2, :], raw(z_hi[:, ct, :]),
                                          ALU.subtract).then_inc(z_lo_ready, 1)
                    if not (is_last(b, B) and u == HB - 1):
                        nu, nb = (u + 1) % HB, b + (u + 1) // HB
                        prepare_ctx(t + 1, nu, nb)
                        prepare_x(t + 1, nu, nb)
                    for ct in range(CT):
                        take_lo(t, 2 * CT + ct, CT + ct)

            repeat(dve, B, body)

        @block.tensor
        def _(pe):
            def product(t, i, lhs, rhs):
                o = OUTS * t + i
                wait_count(pe, act_out, o - 3)
                for ct in range(CT):
                    for n, (a, m) in enumerate(((0, 0), (0, 1), (1, 0))):
                        last = pe.matmul(out_ps[:, i % 4, :], lhs(a, ct), rhs(m, ct),
                                         start=(ct == 0 and n == 0), stop=(ct == CT - 1 and n == 2))
                last.then_inc(out_ready, 1)

            w_kv, w_q, cs, zs = (wkv_hi, wkv_lo), (wq_hi, wq_lo), (c_hi, c_lo), (z_hi, z_lo)

            def body(b):
                for u in range(HB):
                    t = HB * b + u
                    first = isinstance(b, int) and t == 0
                    if first:
                        pe.wait_ge(w_lo_ready, 1)
                    pe.wait_ge(c_lo_ready, t + 1)
                    for i in range(CT):
                        wait_count(pe, dve_out, 2 * CT * t - (CT - 1) + i)
                        product(t, i, lambda a, ct: w_kv[a][:, ct, i * P:(i + 1) * P], lambda m, ct: cs[m][:, ct, :])
                    if first:
                        pe.wait_ge(ident_ready, 2)
                    pe.wait_ge(z_ready, t + 1)
                    for ct in range(CT):
                        wait_count(pe, z_lo_ready, CT * t + ct - 1)
                        for j in range(TT):
                            last = pe.transpose(zT_ps[:, ct % 2, j * P:(j + 1) * P], z[:, j, ct * P:(ct + 1) * P],
                                                ident[:, :])
                        last.then_inc(zT_ready, 1)
                    if first:
                        pe.wait_ge(w_lo_ready, 2)
                    for j in range(TT):
                        pe.wait_ge(dve_out, 2 * CT * t + j + 1)
                        product(t, CT + j, lambda a, ct: cs[a][:, ct, j * P:(j + 1) * P],
                                lambda m, ct: w_kv[m][:, ct, D:2 * D])
                    if first:
                        pe.wait_ge(w_lo_ready, 3)
                    pe.wait_ge(z_lo_ready, CT * (t + 1))
                    for ot in range(CT):
                        product(t, 2 * CT + ot, lambda a, ct: w_q[a][:, ct, ot * P:(ot + 1) * P],
                                lambda m, ct: zs[m][:, ct, :])

            repeat(pe, B, body)


def attention(nc, bias, q_scr, k_scr, v_scr, o_scr, ident, B, T, S, H, DH, INV_SCALE):
    NQ, NKT = T // P, S // P
    TILES = B * NQ
    LAG = 2
    PV0 = NQ + LAG
    NX = 4
    with ExitStack() as c:
        def sb(name, shape, dt=F32):
            return c.enter_context(nc.sbuf_tensor(name, shape, dt))

        def sem(name):
            return c.enter_context(nc.semaphore(name))

        bias_sb = sb("bias_sb", [P, NQ, S])
        q_pack = sb("q_pack", [P, B, T], F32R)
        k_pack = sb("k_pack", [P, B, S], F32R)
        v_ones = sb("v_ones", [P, B, 2 * DH, NKT])
        xs = sb("xs", [P, NX, S])
        row_max = sb("row_max", [P, NX])
        probs = sb("probs", [P, 2, NKT, T])
        o_stage = sb("o_stage", [P, 2, TB])
        scores_ps = c.enter_context(nc.psum_tensor("scores_ps", [P, 2, S], F32))
        xT_ps = c.enter_context(nc.psum_tensor("xT_ps", [P, 2, TB], F32))
        o_ps = c.enter_context(nc.psum_tensor("o_ps", [P, 2, TB], F32))

        pack_loaded = [sem(f"pack_loaded{b}") for b in range(B)]
        v_loaded = [sem(f"v_loaded{b}") for b in range(B)]
        bias_loaded = [sem(f"bias_loaded{i}") for i in range(NQ)]
        ones_ready, scores_ready, biased, shifted = sem("ones_ready"), sem("scores_ready"), sem("biased"), sem("shifted")
        xT_ready, probs_ready, pv_ready, o_taken = sem("xT_ready"), sem("probs_ready"), sem("pv_ready"), sem("o_taken")
        o_stored = [sem(f"o_stored{i}") for i in range(2)]
        block = c.enter_context(nc.Block())

        @block.sync
        def _(sp):
            def load_pack(h, b):
                wait_count(sp, scores_ready, TILES * (h - 1) + NQ * (b + 1))
                for l in range(2):
                    rows = slice(64 * l, 64 * l + 64)
                    sp.dma_start(raw(q_pack[rows, b, :]),
                                 q_scr[b, bass.ds(h * DH, DH), :, :].rearrange("d m t -> (d m) t")
                                 ).then_inc(pack_loaded[b], 16)
                    k_rows = k_scr[b, bass.ds(h * DH, DH), l:l + 1, :]
                    sp.dma_start(raw(k_pack[rows, b, :]), k_rows.broadcast_to([DH, 2, S])).then_inc(pack_loaded[b], 16)

            def load_v(h, b):
                wait_count(sp, pv_ready, B * (h - 1) + b + 1)
                sp.dma_start(v_ones[:, b, 0:DH, :].rearrange("p d k -> p (d k)"), v_scr[b, bass.ds(h, 1), :, :].rearrange("h p n -> (h p) n")
                             ).then_inc(v_loaded[b], 16)

            def load_bias(h, qt):
                wait_count(sp, biased, TILES * (h - 1) + (B - 1) * NQ + qt + 1)
                sp.dma_start(bias_sb[:, qt, :],
                             bias[0, bass.ds(h, 1), qt * P:(qt + 1) * P, :].rearrange("h p s -> (h p) s")
                             ).then_inc(bias_loaded[qt], 16)

            def body(h):
                load_pack(h, 0)
                load_pack(h, 1)
                load_v(h, 0)
                load_pack(h, 2)
                load_bias(h, 0)
                load_bias(h, 1)
                load_v(h, 1)
                for qt in range(2, NQ):
                    load_bias(h, qt)
                load_pack(h, 3)
                load_v(h, 2)
                load_v(h, 3)

            repeat(sp, H, body)

        @block.gpsimd
        def _(pool):
            pool.memset(v_ones[:, :, DH:2 * DH, :], 1.0).then_inc(ones_ready, 1)

            def body(h):
                for j in range(TILES):
                    n = TILES * h + j
                    xb = xs[:, j % NX, :]
                    wait_apart(pool, biased, n + 1)
                    pool.tensor_scalar(xb, xb, -1.0, row_max[:, j % NX:j % NX + 1], ALU.mult, ALU.add
                                       ).then_inc(shifted, 1)

            repeat(pool, H, body)

        @block.vector
        def _(dve):
            def take_output(group, slot):
                dve.wait_ge(pv_ready, group + 1)
                wait_count(dve, o_stored[slot], 16 * (group - slot))
                dve.tensor_copy(o_stage[:, slot, :], o_ps[:, slot, :]).then_inc(o_taken, 1)

            def body(h):
                for j in range(TILES):
                    n = TILES * h + j
                    b, qt = j // NQ, j % NQ
                    if b == 0:
                        dve.wait_ge(bias_loaded[qt], 16 * (h + 1))
                    wait_count(dve, xT_ready, 2 * (n - NX + 1))
                    wait_apart(dve, scores_ready, n + 1)
                    dve.tensor_tensor_reduce(out=xs[:, j % NX, :], in0=scores_ps[:, j % 2, :], in1=bias_sb[:, qt, :],
                                             scale=1.0, scalar=-3.4e38, op0=ALU.add, op1=ALU.max,
                                             accum_out=row_max[:, j % NX:j % NX + 1]).then_inc(biased, 1)
                    if qt == 2 and not (isinstance(h, int) and h == 0 and b < 2):
                        take_output(B * h + b - 2, b % 2)

            repeat(dve, H, body)
            for g in (B * H - 2, B * H - 1):
                take_output(g, g % 2)

        @block.scalar
        def _(act):
            def store_output(group, slot, b, h):
                act.wait_ge(o_taken, group + 1)
                for half in range(2):
                    act.dma_start(o_scr[bass.ds(h, 1), :, b * T + half * TB:b * T + (half + 1) * TB
                                        ].rearrange("h d t -> (h d) t"),
                                  o_stage[64 * half:64 * half + DH + 1, slot, :]).then_inc(o_stored[slot], 16)

            def body(h):
                for j in range(TILES):
                    b, qt = j // NQ, j % NQ
                    if qt == 0:
                        wait_count(act, pv_ready, B * h + b - 1)
                    for half in range(2):
                        act.wait_ge(xT_ready, 2 * (TILES * h + j) + half + 1)
                        act.activation(probs[:, b % 2, half * 4:half * 4 + 4, qt * P:(qt + 1) * P],
                                       xT_ps[:, half, :].rearrange("p (k q) -> p k q", q=P), ACT.Exp,
                                       scale=-INV_SCALE).then_inc(probs_ready, 1)
                    if qt == 2:
                        if b >= 2:
                            store_output(B * h + b - 2, b % 2, b - 2, h)
                        elif not (isinstance(h, int) and h == 0):
                            store_output(B * h + b - 2, b % 2, b + 2, h - 1)

            repeat(act, H, body)
            store_output(B * H - 2, 0, B - 2, H - 1)
            store_output(B * H - 1, 1, B - 1, H - 1)
            for slot in range(2):
                act.wait_ge(o_stored[slot], 16 * B * H)

        @block.tensor
        def _(pe):
            def scores(n, j, h):
                b, qt = j // NQ, j % NQ
                if qt == 0:
                    pe.wait_ge(pack_loaded[b], 64 * (h + 1))
                wait_count(pe, biased, n - 1)
                for half in range(2):
                    last = pe.matmul(scores_ps[:, j % 2, half * TB:(half + 1) * TB],
                                     q_pack[:, b, qt * P:(qt + 1) * P], k_pack[:, b, half * TB:(half + 1) * TB],
                                     start=True, stop=True)
                last.then_inc(scores_ready, 1)

            def transposes(n, j):
                pe.wait_ge(shifted, n + 1)
                for half in range(2):
                    wait_count(pe, probs_ready, 2 * n + half - 1)
                    for k in range(4):
                        kt = 4 * half + k
                        last = pe.transpose(xT_ps[:, half, k * P:(k + 1) * P], xs[:, j % NX, kt * P:(kt + 1) * P],
                                            ident[:, :])
                    last.then_inc(xT_ready, 1)

            def outputs(group, b, kt, h):
                if kt == 0:
                    pe.wait_ge(probs_ready, 2 * NQ * (group + 1))
                    pe.wait_ge(v_loaded[b], 16 * (h + 1))
                    wait_count(pe, o_taken, group - 1)
                    if isinstance(group, int) and group == 0:
                        pe.wait_ge(ones_ready, 1)
                for half in range(2):
                    last = pe.matmul(o_ps[64 * half:64 * half + 64, b % 2, :], v_ones[:, b, :, kt],
                                     probs[:, b % 2, kt, half * TB:(half + 1) * TB],
                                     start=(kt == 0), stop=(kt == NKT - 1))
                if kt == NKT - 1:
                    last.then_inc(pv_ready, 1)

            def outputs_at(h, j):
                back = j - PV0
                h_of = h if back >= 0 else h - 1
                b, kt = (back % TILES) // NQ, back % NQ
                outputs(B * h_of + b, b, kt, h_of)

            def body(h):
                for j in range(TILES):
                    n = TILES * h + j
                    scores(n, j, h)
                    if not (isinstance(h, int) and n < LAG):
                        transposes(n - LAG, (j - LAG) % TILES)
                    if not (isinstance(h, int) and n < PV0):
                        outputs_at(h, j)

            repeat(pe, H, body)
            for j in range(PV0):
                if j < LAG:
                    transposes(TILES * H + j - LAG, TILES + j - LAG)
                outputs_at(H, j)


def project_out(nc, x, g_xattn, Wproj, Wr, br, o_scr, r_scr, x1_scr, z2_scr, ident, experts):
    B, T, D = x.shape
    CT, HB, DH, NE = D // P, T // TB, 32, Wr.shape[1]
    H, HPT = D // DH, P // DH
    NT = B * HB
    with ExitStack() as c:
        def sb(name, shape, dt=F32):
            return c.enter_context(nc.sbuf_tensor(name, shape, dt))

        def sem(name):
            return c.enter_context(nc.semaphore(name))

        sums = sb("sums", [P, TB])
        rsums = sb("rsums", [P, TB])
        wp_raw = sb("wp_raw", [P, CT, D])
        wp_hi, wp_lo = sb("wp_hi", [P, CT, D], F32R), sb("wp_lo", [P, CT, D], F32R)
        wr_sb = sb("wr_sb", [P, CT, NE])
        br_sb = sb("br_sb", [1, NE])
        gate, gate_t = sb("gate", [P, 1]), sb("gate_t", [P, 1])
        o_in = sb("o_in", [P, HB, CT, TB])
        r_in = sb("r_in", [P, HB, CT, TB])
        x_in = sb("x_in3", [P, HB, TT, D])
        y = sb("y", [P, CT, TB])
        y_hi, y_lo = sb("y_hi", [P, CT, TB], F32R), sb("y_lo", [P, CT, TB], F32R)
        x1 = sb("x1", [P, HB, TT, D])
        z2 = sb("z2", [P, TT, D])
        zT = sb("zT", [P, 2, CT, TB], F32R)
        stats = sb("stats3", [P, TT, 6])
        moments = sb("moments3", [P, TT, 2])
        var_eps = sb("var_eps3", [P, TT])
        rstd = sb("rstd3", [P, TT])
        minus_half = sb("minus_half3", [P, TT])
        z_sum = sb("z_sum", [P, CT, B, HB])
        z_tot = sb("z_tot", [P, CT, B])
        route = sb("route", [1, B, NE])
        best = sb("best", [1, B, 8])
        y_ps = c.enter_context(nc.psum_tensor("y_ps", [P, 4, D], F32))
        zT_ps = c.enter_context(nc.psum_tensor("zT_ps3", [P, 2, TB], F32))
        route_ps = c.enter_context(nc.psum_tensor("route_ps", [1, B, NE], F32))

        sums_loaded, rsums_ready, rsums_stored = sem("sums_loaded"), sem("rsums_ready"), sem("rsums_stored")
        wp_loaded, small_loaded = sem("wp_loaded"), sem("small_loaded")
        o_loaded = [sem(f"o_loaded{u}") for u in range(HB)]
        r_loaded = [sem(f"r_loaded{u}") for u in range(HB)]
        x_loaded = [sem(f"x_loaded3{u}") for u in range(HB)]
        wp_hi_ready, wp_ready, gate_ready, const_ready = sem("wp_hi_ready"), sem("wp_ready"), sem("gate_ready"), sem("const3")
        y_ready, y_hi_ready, y_lo_ready, y_done = sem("y_ready"), sem("y_hi_ready"), sem("y_lo_ready"), sem("y_done")
        x1_ready, stats_ready, moments_ready, eps_added = sem("x1_ready"), sem("stats_ready3"), sem("moments3s"), sem("eps3")
        rstd_ready, z_ready, zT_ready = sem("rstd3s"), sem("z_ready3"), sem("zT_ready3")
        z_hi_ready, z_lo_ready = sem("z_hi3"), sem("z_lo3")
        x1_stored = [sem(f"x1_stored{u}") for u in range(HB)]
        z_stored = sem("z_stored")
        tot_ready, route_done, route_ready, best_ready, expert_ready = (
            sem("tot_ready"), sem("route_done"), sem("route_ready"), sem("best_ready"), sem("expert_ready"))
        block = c.enter_context(nc.Block())

        @block.sync
        def _(sp):
            for h in range(H):
                sp.dma_start(sums[h * NT:(h + 1) * NT, :], o_scr[h, DH, :].rearrange("(c t) -> c t", t=TB)
                             ).then_inc(sums_loaded, 16)
            sp.dma_start(wp_raw[:, :, :], Wproj.rearrange("(c p) n -> p c n", p=P)).then_inc(wp_loaded, 16)
            sp.dma_start(wr_sb[:, :, :], Wr.rearrange("(c p) e -> p c e", p=P)).then_inc(small_loaded, 16)
            sp.dma_start(br_sb[:, :], br.rearrange("(a e) -> a e", a=1)).then_inc(small_loaded, 16)
            sp.dma_start(gate[:, :], g_xattn.rearrange("(a e) -> a e", a=1).broadcast_to([P, 1])).then_inc(small_loaded, 16)

            def loads(b):
                for u in range(HB):
                    t = HB * b + u
                    tok = bass.ds(t * TB, TB)
                    wait_count(sp, y_ready, t - 1)
                    for h in range(H):
                        sp.dma_start(o_in[DH * (h % HPT):DH * (h % HPT) + DH, u, h // HPT, :], o_scr[h, 0:DH, tok]
                                     ).then_inc(o_loaded[u], 16)
                    if isinstance(b, int) and t == 0:
                        sp.wait_ge(rsums_ready, 1)
                        sp.dma_start(r_scr.rearrange("h (c t) -> (h c) t", t=TB), rsums[:, :]).then_inc(rsums_stored, 16)
                        sp.wait_ge(rsums_stored, 16)
                    for ct in range(CT):
                        r_rows = r_scr[ct * HPT:(ct + 1) * HPT, tok].rearrange("(h a) t -> h a t", a=1)
                        sp.dma_start(r_in[:, u, ct, :], r_rows.broadcast_to([HPT, DH, TB])).then_inc(r_loaded[u], 16)
                    wait_count(sp, x1_ready, TT * (t - 1))
                    sp.dma_start(x_in[:, u, :, :], x[b, u * TB:(u + 1) * TB, :].rearrange("(j p) n -> p j n", p=P)
                                 ).then_inc(x_loaded[u], 16)

            repeat(sp, B, loads)
            for u in range(HB):
                sp.wait_ge(x1_stored[u], 16 * B)
            sp.wait_ge(z_stored, 32 * NT)

        @block.gpsimd
        def _(pool):
            pool.memset(minus_half[:, :], -0.5).then_inc(const_ready, 1)
            pool.wait_ge(const_ready, 1)

            def normalise(t, u, b):
                pool.wait_ge(o_loaded[u], 16 * H * (b + 1))
                pool.wait_ge(r_loaded[u], 16 * CT * (b + 1))
                wait_count(pool, y_lo_ready, t)
                pool.tensor_tensor(y[:, :, :], o_in[:, u, :, :], r_in[:, u, :, :], ALU.mult).then_inc(y_ready, 1)

            normalise(0, 0, 0)

            def body(b):
                for u in range(HB):
                    t = HB * b + u
                    if not (is_last(b, B) and u == HB - 1):
                        normalise(t + 1, (u + 1) % HB, b + (u + 1) // HB)
                    pool.wait_ge(eps_added, t + 1)
                    wait_count(pool, z_ready, t)
                    pool.tensor_tensor(rstd[:, :], var_eps[:, :], minus_half[:, :], ALU.pow).then_inc(rstd_ready, 1)

            repeat(pool, B, body)

        @block.scalar
        def _(act):
            act.wait_ge(small_loaded, 48)
            act.activation(gate_t[:, :], gate[:, :], ACT.Tanh).then_inc(gate_ready, 1)

            def y_hi_of(t):
                act.wait_ge(y_ready, t + 1)
                wait_count(act, y_done, TT * t)
                act.activation(y_hi[:, :, :], y[:, :, :], ACT.Copy).then_inc(y_hi_ready, 1)

            y_hi_of(0)

            def body(b):
                for u in range(HB):
                    t = HB * b + u
                    if not (is_last(b, B) and u == HB - 1):
                        y_hi_of(t + 1)
                    act.wait_ge(x1_ready, TT * (t + 1))
                    act.dma_start(x1_scr[bass.ds(t * TB, TB), :].rearrange("(j p) n -> p j n", p=P), x1[:, u, :, :]
                                  ).then_inc(x1_stored[u], 16)
                    wait_count(act, z_stored, 32 * t)
                    for ct in range(CT):
                        act.wait_ge(zT_ready, CT * t + ct + 1)
                        act.activation(zT[:, 0, ct, :], zT_ps[:, ct % 2, :], ACT.Copy,
                                       accum_out=z_sum[:, ct, b, u:u + 1] if isinstance(b, int)
                                       else z_sum[:, ct, bass.ds(b, 1), u]).then_inc(z_hi_ready, 1)
                    act.wait_ge(z_lo_ready, CT * (t + 1))
                    for l in range(2):
                        act.dma_start(z2_scr[bass.ds(t, 1), :, l, :, :].rearrange("a p c t -> (a p) c t"),
                                      raw(zT[:, l, :, :])).then_inc(z_stored, 16)

            repeat(act, B, body)

        @block.vector
        def _(dve):
            dve.wait_ge(sums_loaded, 16 * H)
            dve.reciprocal(rsums[:, :], sums[:, :]).then_inc(rsums_ready, 1)
            dve.wait_ge(wp_loaded, 16)
            dve.tensor_copy(wp_hi[:, :, :], wp_raw[:, :, :]).then_inc(wp_hi_ready, 1)
            dve.wait_ge(wp_hi_ready, 1)
            dve.tensor_tensor(wp_lo[:, :, :], wp_raw[:, :, :], raw(wp_hi[:, :, :]), ALU.subtract).then_inc(wp_ready, 1)

            def y_lo_of(t):
                dve.wait_ge(y_hi_ready, t + 1)
                dve.tensor_tensor(y_lo[:, :, :], y[:, :, :], raw(y_hi[:, :, :]), ALU.subtract).then_inc(y_lo_ready, 1)

            y_lo_of(0)
            dve.wait_ge(gate_ready, 1)

            def body(b):
                for u in range(HB):
                    t = HB * b + u
                    dve.wait_ge(x_loaded[u], 16 * (b + 1))
                    wait_count(dve, x1_stored[u], 16 * b)
                    for j in range(TT):
                        dve.wait_ge(y_done, TT * t + j + 1)
                        dve.scalar_tensor_tensor(x1[:, u, j, :], y_ps[:, j, :], gate_t[:, 0:1], x_in[:, u, j, :],
                                                 ALU.mult, ALU.add).then_inc(x1_ready, 1)
                        if j:
                            dve.wait_ge(x1_ready, TT * t + j)
                            dve.bn_stats(stats[:, j - 1, :], x1[:, u, j - 1, :]).then_inc(stats_ready, 1)
                    dve.wait_ge(x1_ready, TT * (t + 1))
                    dve.bn_stats(stats[:, TT - 1, :], x1[:, u, TT - 1, :]).then_inc(stats_ready, 1)
                    wait_apart(dve, stats_ready, TT * (t + 1))
                    for j in range(TT):
                        last = dve.bn_aggr(moments[:, j, :], stats[:, j, :])
                    last.then_inc(moments_ready, 1)
                    dve.wait_ge(moments_ready, t + 1)
                    dve.tensor_scalar(var_eps[:, :], moments[:, :, 1], EPS, None, ALU.add).then_inc(eps_added, 1)
                    if not (is_last(b, B) and u == HB - 1):
                        y_lo_of(t + 1)
                    dve.wait_ge(rstd_ready, t + 1)
                    wait_count(dve, zT_ready, CT * t)
                    for j in range(TT):
                        last = dve.tensor_scalar(z2[:, j, :], x1[:, u, j, :], moments[:, j, 0:1], rstd[:, j:j + 1],
                                                 ALU.subtract, ALU.mult)
                    last.then_inc(z_ready, 1)
                    for ct in range(CT):
                        dve.wait_ge(z_hi_ready, CT * t + ct + 1)
                        dve.tensor_tensor(zT[:, 1, ct, :], zT_ps[:, ct % 2, :], raw(zT[:, 0, ct, :]),
                                          ALU.subtract).then_inc(z_lo_ready, 1)

            repeat(dve, B, body)
            dve.wait_ge(z_hi_ready, CT * NT)
            dve.tensor_tensor(z_tot[:, :, :], z_sum[:, :, :, 0], z_sum[:, :, :, 1], ALU.add).then_inc(tot_ready, 1)
            dve.wait_ge(route_done, 1)
            dve.wait_ge(small_loaded, 48)
            for b in range(B):
                last = dve.scalar_tensor_tensor(route[:, b, :], route_ps[:, b, :], 1.0 / T, br_sb[:, :],
                                                ALU.mult, ALU.add)
            last.then_inc(route_ready, 1)
            dve.wait_ge(route_ready, 1)
            for b in range(B):
                last = dve.max(best[:, b, :], route[:, b, :])
            last.then_inc(best_ready, 1)
            dve.wait_ge(best_ready, 1)
            for b in range(B):
                last = dve.max_index(experts[:, b, :], best[:, b, :], route[:, b, :])
            last.then_inc(expert_ready, 1)

        @block.tensor
        def _(pe):
            def products(t):
                for j in range(TT):
                    wait_count(pe, x1_ready, TT * (t - 1) + j + 1)
                    for ct in range(CT):
                        for n, (a, w) in enumerate(((y_hi, wp_hi), (y_hi, wp_lo), (y_lo, wp_hi))):
                            last = pe.matmul(y_ps[:, j, :], a[:, ct, j * P:(j + 1) * P], w[:, ct, :],
                                             start=(ct == 0 and n == 0), stop=(ct == CT - 1 and n == 2))
                    last.then_inc(y_done, 1)

            pe.wait_ge(wp_ready, 1)
            pe.wait_ge(y_lo_ready, 1)
            products(0)

            def body(b):
                for u in range(HB):
                    t = HB * b + u
                    if not (is_last(b, B) and u == HB - 1):
                        pe.wait_ge(y_lo_ready, t + 2)
                        products(t + 1)
                    pe.wait_ge(z_ready, t + 1)
                    for ct in range(CT):
                        wait_count(pe, z_lo_ready, CT * t + ct - 1)
                        for j in range(TT):
                            last = pe.transpose(zT_ps[:, ct % 2, j * P:(j + 1) * P], z2[:, j, ct * P:(ct + 1) * P],
                                                ident[:, :])
                        last.then_inc(zT_ready, 1)

            repeat(pe, B, body)
            pe.wait_ge(tot_ready, 1)
            pe.wait_ge(small_loaded, 48)
            for b in range(B):
                for ct in range(CT):
                    last = pe.matmul(route_ps[:, b, :], z_tot[:, ct, b:b + 1], wr_sb[:, ct, :],
                                     start=(ct == 0), stop=(ct == CT - 1))
            last.then_inc(route_done, 1)


def expert_ffn(nc, g_ffn, W1c, b1c, W2, b2, x1_scr, z2_scr, experts, out, B, T):
    NE, NF, _, D = W1c.shape
    CT, HB = D // P, T // TB
    NW = 4
    with ExitStack() as c:
        def sb(name, shape, dt=F32):
            return c.enter_context(nc.sbuf_tensor(name, shape, dt))

        def sem(name):
            return c.enter_context(nc.semaphore(name))

        w_raw = sb("w_raw", [P, NW, 2, D])
        w_hi, w_lo = sb("w_hi", [P, NW, 2, D], F32R), sb("w_lo", [P, NW, 2, D], F32R)
        zT = sb("zT4", [P, HB, 2, CT, TB], F32R)
        h_full = sb("h_full", [P, 2, TB])
        h_hi, h_lo = sb("h_hi", [P, 2, TB], F32R), sb("h_lo", [P, 2, TB], F32R)
        x1 = sb("x14", [P, HB, TT, D])
        b1_sb = sb("b1_sb", [P, B, NF])
        b2_sb = sb("b2_sb", [P, B, D])
        b2_gated = sb("b2_gated", [P, D])
        gate, gate_t = sb("gate4", [P, 1]), sb("gate_t4", [P, 1])
        h_ps = c.enter_context(nc.psum_tensor("h_ps", [P, 2, TB], F32))
        y_ps = c.enter_context(nc.psum_tensor("y_ps4", [P, TT, D], F32))

        w_loaded = [sem(f"w_loaded{i}") for i in range(NW)]
        z_loaded = [sem(f"z_loaded{u}") for u in range(HB)]
        x1_loaded = [sem(f"x1_loaded{u}") for u in range(HB)]
        b_loaded = sem("b_loaded")
        gate_loaded, gate_ready, b2_ready, x1_biased = sem("gate_loaded"), sem("gate_ready4"), sem("b2_ready"), sem("x1_biased")
        w_hi_ready, w_lo_ready = sem("w_hi4"), sem("w_lo4")
        hT_ready, h_full_ready, h_hi_ready, h_lo_ready = sem("hT_ready"), sem("h_full_ready"), sem("h_hi4"), sem("h_lo4")
        chunk_done, y_done, res_ready = sem("chunk_done"), sem("y_done4"), sem("res_ready")
        out_stored = [sem(f"out_stored{u}") for u in range(HB)]
        block = c.enter_context(nc.Block())

        @block.sync
        def _(sp):
            sp.dma_start(gate[:, :], g_ffn.rearrange("(a e) -> a e", a=1).broadcast_to([P, 1])).then_inc(gate_loaded, 16)

            def body(b):
                e = sp.value_load(experts[0:1, bass.ds(b, 1), 0:1].rearrange("p a e -> p (a e)"), min_val=0, max_val=NE - 1)
                sp.dma_start(b1_sb[:, bass.ds(b, 1), :], b1c[bass.ds(e, 1), :, :].rearrange("a p f -> p a f")
                             ).then_inc(b_loaded, 16)
                sp.dma_start(b2_sb[:, bass.ds(b, 1), :], b2[bass.ds(e, 1), :].rearrange("(c a) n -> c a n", c=1
                                                                                       ).broadcast_to([P, 1, D])
                             ).then_inc(b_loaded, 16)
                sp.wait_ge(b_loaded, 32 * (b + 1))
                for u in range(HB):
                    t = HB * b + u
                    wait_count(sp, chunk_done, NF * (t - 1))
                    sp.dma_start(zT_raw(zT, u), z2_scr[bass.ds(t, 1), :, :, :, :].rearrange("a p l c t -> (a p) (l c t)")
                                 ).then_inc(z_loaded[u], 16)
                    for f in range(NF):
                        slot = f % NW
                        wait_count(sp, w_lo_ready, NF * t + f - NW + 1)
                        sp.dma_start(w_raw[:, slot, 0, :], W1c[bass.ds(e, 1), f, :, :].rearrange("a p n -> (a p) n")
                                     ).then_inc(w_loaded[slot], 16)
                        sp.dma_start(w_raw[:, slot, 1, :], W2[bass.ds(e, 1), f * P:(f + 1) * P, :
                                                             ].rearrange("a p n -> (a p) n")
                                     ).then_inc(w_loaded[slot], 16)
                        if f == NW:
                            wait_count(sp, out_stored[u], 16 * b)
                            sp.dma_start(x1[:, u, :, :], x1_scr[bass.ds(t * TB, TB), :
                                                               ].rearrange("(j p) n -> p j n", p=P)
                                         ).then_inc(x1_loaded[u], 16)

            repeat(sp, B, body)

        @block.gpsimd
        def _(pool):
            pool.wait_ge(gate_ready, 1)

            def body(b):
                pool.wait_ge(b_loaded, 32 * (b + 1))
                wait_count(pool, x1_biased, HB * b)
                pool.tensor_tensor(b2_gated[:, :], b2_sb[:, bass.ds(b, 1), :].rearrange("p a n -> p (a n)"),
                                   gate_t[:, 0:1].broadcast_to([P, D]), ALU.mult).then_inc(b2_ready, 1)
                pool.wait_ge(b2_ready, b + 1)
                for u in range(HB):
                    t = HB * b + u
                    pool.wait_ge(x1_loaded[u], 16 * (b + 1))
                    for j in range(TT):
                        last = pool.tensor_tensor(x1[:, u, j, :], x1[:, u, j, :], b2_gated[:, :], ALU.add)
                    last.then_inc(x1_biased, 1)

            repeat(pool, B, body)

        @block.scalar
        def _(act):
            act.wait_ge(gate_loaded, 16)
            act.activation(gate_t[:, :], gate[:, :], ACT.Tanh).then_inc(gate_ready, 1)

            def store(t, u):
                act.wait_ge(res_ready, TT * (t + 1))
                act.dma_start(out[bass.ds(t * TB, TB), :].rearrange("(j p) n -> p j n", p=P), x1[:, u, :, :]
                              ).then_inc(out_stored[u], 16)

            def body(b):
                act.wait_ge(b_loaded, 32 * (b + 1))
                for u in range(HB):
                    t = HB * b + u
                    for f in range(NF):
                        n = NF * t + f
                        b1 = b1_sb[:, bass.ds(b, 1), f:f + 1].rearrange("p a f -> p (a f)")
                        wait_count(act, h_lo_ready, n - 1)
                        wait_apart(act, hT_ready, n + 1)
                        act.activation(h_full[:, f % 2, :], h_ps[:, f % 2, :], ACT.Relu, bias=b1
                                       ).then_inc(h_full_ready, 1)
                        if not (isinstance(n, int) and n < 2):
                            wait_apart(act, chunk_done, n - 1)
                        act.activation(h_hi[:, f % 2, :], h_ps[:, f % 2, :], ACT.Relu, bias=b1).then_inc(h_hi_ready, 1)
                        if f == 2 and not (isinstance(t, int) and t == 0):
                            store(t - 1, (u + 1) % HB)

            repeat(act, B, body)
            store(B * HB - 1, HB - 1)
            for u in range(HB):
                act.wait_ge(out_stored[u], 16 * B)

        @block.vector
        def _(dve):
            def split_chunk(n, f, count):
                slot = f % NW
                dve.wait_ge(w_loaded[slot], 32 * count)
                wait_count(dve, chunk_done, n - NW + 1)
                dve.tensor_copy(w_hi[:, slot, :, :], w_raw[:, slot, :, :]).then_inc(w_hi_ready, 1)
                dve.wait_ge(w_hi_ready, n + 1)
                dve.tensor_tensor(w_lo[:, slot, :, :], w_raw[:, slot, :, :], raw(w_hi[:, slot, :, :]), ALU.subtract
                                  ).then_inc(w_lo_ready, 1)

            split_chunk(0, 0, 1)
            split_chunk(1, 1, 1)

            def body(b):
                for u in range(HB):
                    t = HB * b + u
                    for f in range(NF):
                        n = NF * t + f
                        dve.wait_ge(h_hi_ready, n + 1)
                        dve.tensor_tensor(h_lo[:, f % 2, :], h_full[:, f % 2, :], raw(h_hi[:, f % 2, :]), ALU.subtract
                                          ).then_inc(h_lo_ready, 1)
                        if not (is_last(b, B) and u == HB - 1 and f >= NF - 2):
                            f2 = (f + 2) % NF
                            split_chunk(n + 2, f2, (NF // NW) * (t + (f + 2) // NF) + f2 // NW + 1)
                    dve.wait_ge(x1_biased, t + 1)
                    for j in range(TT):
                        if j < TT - 1:
                            dve.wait_ge(y_done, (TT - 1) * t + j + 1)
                        else:
                            dve.wait_ge(chunk_done, NF * (t + 1))
                        dve.scalar_tensor_tensor(x1[:, u, j, :], y_ps[:, j, :], gate_t[:, 0:1], x1[:, u, j, :],
                                                 ALU.mult, ALU.add).then_inc(res_ready, 1)

            dve.wait_ge(gate_ready, 1)
            repeat(dve, B, body)

        @block.tensor
        def _(pe):
            def hidden(t, b, u, f):
                n = NF * t + f
                if f == 0:
                    pe.wait_ge(z_loaded[u], 16 * (b + 1))
                pe.wait_ge(w_lo_ready, n + 1)
                wait_count(pe, h_hi_ready, n - 1)
                for ct in range(CT):
                    cs = slice(ct * P, (ct + 1) * P)
                    for i, (w, l) in enumerate(((w_hi, 0), (w_hi, 1), (w_lo, 0))):
                        last = pe.matmul(h_ps[:, f % 2, :], w[:, f % NW, 0, cs], zT[:, u, l, ct, :],
                                         start=(ct == 0 and i == 0), stop=(ct == CT - 1 and i == 2))
                last.then_inc(hT_ready, 1)

            def result(t, f):
                n = NF * t + f
                pe.wait_ge(h_lo_ready, n + 1)
                for j in range(TT):
                    if f == 0:
                        wait_count(pe, res_ready, TT * (t - 1) + j + 1)
                    js = slice(j * P, (j + 1) * P)
                    for i, (a, w) in enumerate(((h_hi, w_hi), (h_hi, w_lo), (h_lo, w_hi))):
                        last = pe.matmul(y_ps[:, j, :], a[:, f % 2, js], w[:, f % NW, 1, :],
                                         start=(f == 0 and i == 0), stop=(f == NF - 1 and i == 2))
                    if f == NF - 1 and j < TT - 1:
                        last.then_inc(y_done, 1)
                last.then_inc(chunk_done, 1)

            hidden(0, 0, 0, 0)

            def body(b):
                for u in range(HB):
                    t = HB * b + u
                    for f in range(NF):
                        if f < NF - 1:
                            hidden(t, b, u, f + 1)
                        elif not (is_last(b, B) and u == HB - 1):
                            hidden(t + 1, b + (u + 1) // HB, (u + 1) % HB, 0)
                        result(t, f)

            repeat(pe, B, body)


def zT_raw(zT, u):
    return raw(zT[:, u, :, :, :]).rearrange("p l c t -> p (l c t)")



def kernel(x, ctx_1024, g_xattn, g_ffn, L0_xattn_position_bias, L0_xattn_W_q, L0_xattn_W_kv, L0_xattn_W_proj,
           L0_ffn_Wr, L0_ffn_br, L0_ffn_W1, L0_ffn_b1, L0_ffn_W2, L0_ffn_b2):
    import numpy as np
    import concourse.bacc as bacc
    from concourse import mybir as mb
    from concourse.bass_utils import run_bass_kernel_spmd

    W1, b1 = np.asarray(L0_ffn_W1), np.asarray(L0_ffn_b1)
    E, D, F = W1.shape
    arrays = {
        "x": x,
        "ctxT": np.asarray(ctx_1024).transpose(0, 2, 1),
        "g_xattn": g_xattn,
        "g_ffn": g_ffn,
        "bias": L0_xattn_position_bias,
        "Wq": L0_xattn_W_q,
        "Wkv": L0_xattn_W_kv,
        "Wproj": L0_xattn_W_proj,
        "Wr": L0_ffn_Wr,
        "br": L0_ffn_br,
        "W1c": W1.reshape(E, D // 128, 128, F // 128, 128).transpose(0, 3, 2, 1, 4).reshape(E, F // 128, 128, D),
        "b1c": b1.reshape(E, F // 128, 128).transpose(0, 2, 1),
        "W2": L0_ffn_W2,
        "b2": L0_ffn_b2,
    }
    arrays = {k: np.ascontiguousarray(v) for k, v in arrays.items()}
    nc = bacc.Bacc("TRN2", target_bir_lowering=False, num_devices=1)
    ins = [nc.dram_tensor(k, v.shape, mb.dt.from_np(v.dtype), kind="ExternalInput").ap() for k, v in arrays.items()]
    shape = tuple(np.asarray(x).shape)
    out = nc.dram_tensor("out", (shape[0] * shape[1], shape[2]), mb.dt.float32, kind="ExternalOutput").ap()
    gated_block(nc, *ins, out)
    r = run_bass_kernel_spmd(nc, [arrays], core_ids=[0])
    return r.results[0]["out"].reshape(shape)
```

```python
import concourse.bass as bass
from concourse import mybir
from contextlib import ExitStack

F32 = mybir.dt.float32
F32R = mybir.dt.float32r
U32 = mybir.dt.uint32
ALU = mybir.AluOpType
ACT = mybir.ActivationFunctionType
AX = mybir.AxisListType

P = 128
TB = 512
TT = TB // P
EPS = 1e-5


def wait_count(eng, sem, n):
    if not (isinstance(n, int) and n <= 0):
        eng.wait_ge(sem, n)


def wait_apart(eng, sem, n):
    if isinstance(n, int):
        eng.wait_ge(sem, n)
    else:
        count = eng.to_reg(n)
        eng.wait_ge(sem, 1)
        eng.wait_ge(sem, count)


def repeat(eng, n, body):
    body(0)
    with eng.Fori(1, n - 1) as i:
        body(i)
    body(n - 1)


def is_last(i, n):
    return isinstance(i, int) and i == n - 1


def raw(ap):
    return ap.bitcast(F32)


def gated_block(nc, x, ctxT, g_xattn, g_ffn, bias, Wq, Wkv, Wproj, Wr, br, W1c, b1c, W2, b2, out):
    B, T, D = x.shape
    H = bias.shape[1]
    DH = D // H
    S = ctxT.shape[2]
    NE, NF, _, CTF = W1c.shape
    CT = D // P
    HB = T // TB
    NQ = T // P
    NKT = S // P
    INV_SCALE = float(DH) ** 0.5
    assert (D, DH, T, S, HB, CTF) == (CT * P, 32, NQ * P, T, 2, CT * P)

    q_scr = nc.dram_tensor("q_scr", (B, D, 2, T), F32, kind="Internal").ap()
    k_scr = nc.dram_tensor("k_scr", (B, D, 2, S), F32, kind="Internal").ap()
    v_scr = nc.dram_tensor("v_scr", (B, H, P, NKT * DH), F32, kind="Internal").ap()
    y_scr = nc.dram_tensor("y_scr", (B, 4, D, T // 4), F32, kind="Internal").ap()
    x1_scr = nc.dram_tensor("x1_scr", (B * T, D), F32, kind="Internal").ap()
    z2_scr = nc.dram_tensor("z2_scr", (B * HB, P, CT, TB), F32, kind="Internal").ap()

    with ExitStack() as top:
        ident = top.enter_context(nc.sbuf_tensor("ident", [P, P], F32))
        experts = top.enter_context(nc.sbuf_tensor("experts", [1, B, 8], U32))
        project_qkv(nc, x, ctxT, Wq, Wkv, q_scr, k_scr, v_scr, ident)
        attention(nc, bias, q_scr, k_scr, v_scr, y_scr, ident, B, T, S, H, DH, INV_SCALE)
        project_out(nc, x, g_xattn, Wproj, Wr, br, y_scr, x1_scr, z2_scr, ident, experts)
        expert_ffn(nc, g_ffn, W1c, b1c, W2, b2, x1_scr, z2_scr, experts, out, B, T)


def project_qkv(nc, x, ctxT, Wq, Wkv, q_scr, k_scr, v_scr, ident):
    B, T, D = x.shape
    CT, HB, DH = D // P, T // TB, 32
    H = D // DH
    OUTS = 3 * CT
    with ExitStack() as c:
        def sb(name, shape, dt=F32):
            return c.enter_context(nc.sbuf_tensor(name, shape, dt))

        def sem(name):
            return c.enter_context(nc.semaphore(name))

        wq_raw = sb("wq_raw", [P, CT, D])
        wkv_raw = sb("wkv_raw", [P, CT, 2 * D])
        wq_hi, wq_lo = sb("wq_hi", [P, CT, D], F32R), sb("wq_lo", [P, CT, D], F32R)
        wkv_hi, wkv_lo = sb("wkv_hi", [P, CT, 2 * D], F32R), sb("wkv_lo", [P, CT, 2 * D], F32R)
        xin = sb("xin", [P, HB, TT, D])
        cin = sb("cin", [P, HB, CT, TB])
        c_hi, c_lo = sb("c_hi", [P, CT, TB], F32R), sb("c_lo", [P, CT, TB], F32R)
        z = sb("z", [P, TT, D])
        z_hi, z_lo = sb("z_hi", [P, CT, TB], F32R), sb("z_lo", [P, CT, TB], F32R)
        qk_out = sb("qk_out", [P, 4, 2, TB], F32R)
        v_out = sb("v_out", [P, H, HB * TT, DH])
        stats = sb("stats", [P, TT, 6])
        moments = sb("moments", [P, TT, 2])
        var_eps = sb("var_eps", [P, TT])
        rstd = sb("rstd", [P, TT])
        minus_half = sb("minus_half", [P, TT])
        zT_ps = c.enter_context(nc.psum_tensor("zT_ps", [P, 2, TB], F32))
        out_ps = c.enter_context(nc.psum_tensor("out_ps", [P, 4, TB], F32))

        wkv_loaded, wq_loaded = sem("wkv_loaded"), sem("wq_loaded")
        x_loaded = [sem(f"x_loaded{u}") for u in range(HB)]
        c_loaded = [sem(f"c_loaded{u}") for u in range(HB)]
        w_hi_ready, w_lo_ready = sem("w_hi_ready"), sem("w_lo_ready")
        ident_ready, const_ready = sem("ident_ready"), sem("const_ready")
        c_hi_ready, c_lo_ready = sem("c_hi_ready"), sem("c_lo_ready")
        stats_ready, moments_ready, rstd_ready = sem("stats_ready"), sem("moments_ready"), sem("rstd_ready")
        eps_added = sem("eps_added")
        z_ready, zT_ready, z_hi_ready, z_lo_ready = sem("z_ready"), sem("zT_ready"), sem("z_hi_ready"), sem("z_lo_ready")
        out_ready = sem("out_ready")
        act_out, dve_out = sem("act_out"), sem("dve_out")
        qk_stored = [sem(f"qk_stored{i}") for i in range(4)]
        v_stored = sem("v_stored")

        block = c.enter_context(nc.Block())

        @block.sync
        def _(sp):
            sp.dma_start(wkv_raw[:, :, :], Wkv.rearrange("(c p) n -> p c n", p=P)).then_inc(wkv_loaded, 16)

            def loads(b):
                for u in range(HB):
                    t = HB * b + u
                    wait_count(sp, c_lo_ready, t - 1)
                    sp.dma_start(cin[:, u, :, :], ctxT[b, :, u * TB:(u + 1) * TB].rearrange("(c p) t -> p c t", p=P)
                                 ).then_inc(c_loaded[u], 16)
                    wait_count(sp, z_ready, t - 1)
                    sp.dma_start(xin[:, u, :, :], x[b, u * TB:(u + 1) * TB, :].rearrange("(j p) n -> p j n", p=P)
                                 ).then_inc(x_loaded[u], 16)
                    if isinstance(b, int) and t == 0:
                        sp.dma_start(wq_raw[:, :, :], Wq.rearrange("(c p) n -> p c n", p=P)).then_inc(wq_loaded, 16)

            repeat(sp, B, loads)

        @block.gpsimd
        def _(pool):
            pool.memset(ident[:, :], 0.0).then_inc(ident_ready, 1)
            pool.memset(minus_half[:, :], -0.5).then_inc(const_ready, 1)
            pool.wait_ge(ident_ready, 1)
            pool.affine_select(out=ident[:, :], in_=ident[:, :], compare_op=ALU.not_equal, fill=1.0,
                               base=0, pattern=[[-1, P]], channel_multiplier=1).then_inc(ident_ready, 1)
            pool.wait_ge(const_ready, 1)

            def body(b):
                for u in range(HB):
                    t = HB * b + u
                    pool.wait_ge(c_hi_ready, t + 1)
                    pool.tensor_tensor(c_lo[:, :, :], cin[:, u, :, :], raw(c_hi[:, :, :]), ALU.subtract
                                       ).then_inc(c_lo_ready, 1)
                    pool.wait_ge(eps_added, t + 1)
                    wait_count(pool, z_ready, t)
                    pool.tensor_tensor(rstd[:, :], var_eps[:, :], minus_half[:, :], ALU.pow).then_inc(rstd_ready, 1)

            repeat(pool, B, body)

        @block.scalar
        def _(act):
            def take_hi(t, i, s):
                slot = s % 4
                wait_count(act, qk_stored[slot], 16 * (2 * t + s // 4))
                act.wait_ge(out_ready, OUTS * t + i + 1)
                act.activation(qk_out[:, slot, 0, :], out_ps[:, i % 4, :], ACT.Copy).then_inc(act_out, 1)

            def store(scr, t, b, u, ct, s):
                slot = s % 4
                act.wait_ge(dve_out, 2 * CT * t + s + 1)
                act.dma_start(scr[b, ct * P:(ct + 1) * P, :, u * TB:(u + 1) * TB], raw(qk_out[:, slot, :, :])
                              ).then_inc(qk_stored[slot], 16)

            def body(b):
                for u in range(HB):
                    t = HB * b + u
                    for i in range(CT):
                        take_hi(t, i, i)
                        if i:
                            store(k_scr, t, b, u, i - 1, i - 1)
                    for ct in range(CT):
                        act.wait_ge(zT_ready, CT * t + ct + 1)
                        act.activation(z_hi[:, ct, :], zT_ps[:, ct % 2, :], ACT.Copy).then_inc(z_hi_ready, 1)
                        if ct == 0:
                            store(k_scr, t, b, u, CT - 1, CT - 1)
                    wait_count(act, v_stored, 16 * b)
                    for j in range(TT):
                        i = CT + j
                        act.wait_ge(out_ready, OUTS * t + i + 1)
                        act.activation(v_out[:, :, u * TT + j, :], out_ps[:, i % 4, :].rearrange("p (h d) -> p h d", h=H),
                                       ACT.Copy).then_inc(act_out, 1)
                    if u == HB - 1:
                        act.wait_ge(act_out, OUTS * t + 2 * CT)
                        act.dma_start(v_scr[b, :, :, :].rearrange("h p n -> p h n"),
                                      v_out[:, :, :, :].rearrange("p h j d -> p h (j d)")).then_inc(v_stored, 16)
                    for ct in range(CT):
                        take_hi(t, 2 * CT + ct, CT + ct)
                        if ct:
                            store(q_scr, t, b, u, ct - 1, CT + ct - 1)
                    store(q_scr, t, b, u, CT - 1, 2 * CT - 1)

            repeat(act, B, body)
            for i in range(4):
                act.wait_ge(qk_stored[i], 16 * 2 * B * HB)
            act.wait_ge(v_stored, 16 * B)

        @block.vector
        def _(dve):
            def split_weight(hi, lo, w):
                n = split_weight.n = split_weight.n + 1
                dve.tensor_copy(hi, w).then_inc(w_hi_ready, 1)
                dve.wait_ge(w_hi_ready, n)
                dve.tensor_tensor(lo, w, raw(hi), ALU.subtract).then_inc(w_lo_ready, 1)
            split_weight.n = 0

            def prepare_ctx(t, u, b):
                dve.wait_ge(c_loaded[u], 16 * (b + 1))
                wait_count(dve, out_ready, OUTS * t - CT)
                dve.tensor_copy(c_hi[:, :, :], cin[:, u, :, :]).then_inc(c_hi_ready, 1)

            def prepare_x(t, u, b):
                dve.wait_ge(x_loaded[u], 16 * (b + 1))
                for j in range(TT):
                    last = dve.bn_stats(stats[:, j, :], xin[:, u, j, :])
                last.then_inc(stats_ready, 1)
                wait_apart(dve, stats_ready, t + 1)
                for j in range(TT):
                    last = dve.bn_aggr(moments[:, j, :], stats[:, j, :])
                last.then_inc(moments_ready, 1)
                dve.wait_ge(moments_ready, t + 1)
                wait_count(dve, rstd_ready, t)
                dve.tensor_scalar(var_eps[:, :], moments[:, :, 1], EPS, None, ALU.add).then_inc(eps_added, 1)
                dve.wait_ge(rstd_ready, t + 1)
                wait_count(dve, zT_ready, CT * t)
                for j in range(TT):
                    last = dve.tensor_scalar(z[:, j, :], xin[:, u, j, :], moments[:, j, 0:1], rstd[:, j:j + 1],
                                             ALU.subtract, ALU.mult)
                last.then_inc(z_ready, 1)

            def take_lo(t, i, s):
                dve.wait_ge(act_out, OUTS * t + i + 1)
                dve.tensor_tensor(qk_out[:, s % 4, 1, :], out_ps[:, i % 4, :], raw(qk_out[:, s % 4, 0, :]),
                                  ALU.subtract).then_inc(dve_out, 1)

            dve.wait_ge(wkv_loaded, 16)
            split_weight(wkv_hi[:, :, 0:D], wkv_lo[:, :, 0:D], wkv_raw[:, :, 0:D])
            prepare_ctx(0, 0, 0)
            split_weight(wkv_hi[:, :, D:2 * D], wkv_lo[:, :, D:2 * D], wkv_raw[:, :, D:2 * D])
            prepare_x(0, 0, 0)
            dve.wait_ge(wq_loaded, 16)
            split_weight(wq_hi[:, :, :], wq_lo[:, :, :], wq_raw[:, :, :])

            def body(b):
                for u in range(HB):
                    t = HB * b + u
                    for i in range(CT):
                        take_lo(t, i, i)
                    for ct in range(CT):
                        dve.wait_ge(z_hi_ready, CT * t + ct + 1)
                        dve.tensor_tensor(z_lo[:, ct, :], zT_ps[:, ct % 2, :], raw(z_hi[:, ct, :]),
                                          ALU.subtract).then_inc(z_lo_ready, 1)
                    if not (is_last(b, B) and u == HB - 1):
                        nu, nb = (u + 1) % HB, b + (u + 1) // HB
                        prepare_ctx(t + 1, nu, nb)
                        prepare_x(t + 1, nu, nb)
                    for ct in range(CT):
                        take_lo(t, 2 * CT + ct, CT + ct)

            repeat(dve, B, body)

        @block.tensor
        def _(pe):
            def product(t, i, lhs, rhs):
                o = OUTS * t + i
                wait_count(pe, act_out, o - 3)
                for ct in range(CT):
                    for n, (a, m) in enumerate(((0, 0), (0, 1), (1, 0))):
                        last = pe.matmul(out_ps[:, i % 4, :], lhs(a, ct), rhs(m, ct),
                                         start=(ct == 0 and n == 0), stop=(ct == CT - 1 and n == 2))
                last.then_inc(out_ready, 1)

            w_kv, w_q, cs, zs = (wkv_hi, wkv_lo), (wq_hi, wq_lo), (c_hi, c_lo), (z_hi, z_lo)

            def body(b):
                for u in range(HB):
                    t = HB * b + u
                    first = isinstance(b, int) and t == 0
                    if first:
                        pe.wait_ge(w_lo_ready, 1)
                    pe.wait_ge(c_lo_ready, t + 1)
                    for i in range(CT):
                        wait_count(pe, dve_out, 2 * CT * t - (CT - 1) + i)
                        product(t, i, lambda a, ct: w_kv[a][:, ct, i * P:(i + 1) * P], lambda m, ct: cs[m][:, ct, :])
                    if first:
                        pe.wait_ge(ident_ready, 2)
                    pe.wait_ge(z_ready, t + 1)
                    for ct in range(CT):
                        wait_count(pe, z_lo_ready, CT * t + ct - 1)
                        for j in range(TT):
                            last = pe.transpose(zT_ps[:, ct % 2, j * P:(j + 1) * P], z[:, j, ct * P:(ct + 1) * P],
                                                ident[:, :])
                        last.then_inc(zT_ready, 1)
                    if first:
                        pe.wait_ge(w_lo_ready, 2)
                    for j in range(TT):
                        pe.wait_ge(dve_out, 2 * CT * t + j + 1)
                        product(t, CT + j, lambda a, ct: cs[a][:, ct, j * P:(j + 1) * P],
                                lambda m, ct: w_kv[m][:, ct, D:2 * D])
                    if first:
                        pe.wait_ge(w_lo_ready, 3)
                    pe.wait_ge(z_lo_ready, CT * (t + 1))
                    for ot in range(CT):
                        product(t, 2 * CT + ot, lambda a, ct: w_q[a][:, ct, ot * P:(ot + 1) * P],
                                lambda m, ct: zs[m][:, ct, :])

            repeat(pe, B, body)


def attention(nc, bias, q_scr, k_scr, v_scr, y_scr, ident, B, T, S, H, DH, INV_SCALE):
    NQ, NKT = T // P, S // P
    TILES = B * NQ
    LAG = 5
    ACT_LAG, DVE_LAG = 4, 6
    PV0 = NQ + LAG + 0
    NX = 8
    QW = T // 4
    with ExitStack() as c:
        def sb(name, shape, dt=F32):
            return c.enter_context(nc.sbuf_tensor(name, shape, dt))

        def sem(name):
            return c.enter_context(nc.semaphore(name))

        bias_sb = sb("bias_sb", [P, NQ, S])
        q_pack = sb("q_pack", [P, B, T], F32R)
        k_pack = sb("k_pack", [P, B, S], F32R)
        v_sb = sb("v_sb", [P, B, NKT, DH])
        xs = sb("xs", [P, NX, S])
        row_max, exp_bias = sb("row_max", [P, NX]), sb("exp_bias", [P, NX])
        row_sum, inv_sum = sb("row_sum", [P, NX]), sb("inv_sum", [P, NX])
        probsT = sb("probsT", [P, 2, NKT, T])
        y_stage = sb("y_stage", [P, 2, QW])
        scores_ps = c.enter_context(nc.psum_tensor("scores_ps", [P, 2, S], F32))
        pT_ps = c.enter_context(nc.psum_tensor("pT_ps", [P, 3, TB], F32))
        y_ps = c.enter_context(nc.psum_tensor("y_ps2", [P, TB], F32))

        pack_loaded = [sem(f"pack_loaded{b}") for b in range(B)]
        v_loaded = [sem(f"v_loaded{b}") for b in range(B)]
        bias_loaded = [sem(f"bias_loaded{i}") for i in range(NQ)]
        scores_ready, biased, exp_bias_ready = sem("scores_ready"), sem("biased"), sem("exp_bias_ready")
        exp_ready, inverted, normalised, pT_ready = sem("exp_ready"), sem("inverted"), sem("normalised"), sem("pT_ready")
        dve_copied, act_copied = sem("dve_copied"), sem("act_copied")
        pv_ready, y_taken = sem("pv_ready"), sem("y_taken")
        y_stored = [sem(f"y_stored{i}") for i in range(2)]
        block = c.enter_context(nc.Block())

        def pT_bank(j, half):
            return 2 if half else j % 2

        def copy_half(eng, copy, done, h, j, lag, half):
            if isinstance(h, int) and TILES * h + j < lag:
                return
            n, jt = TILES * h + j - lag, (j - lag) % TILES
            b, qt = jt // NQ, jt % NQ
            if qt == 0:
                wait_count(eng, pv_ready, (B * h + b - 1) if j >= lag else (B * (h - 1) + b - 1))
            eng.wait_ge(pT_ready, 2 * n + half + 1)
            copy(probsT[:, b % 2, half * 4:half * 4 + 4, qt * P:(qt + 1) * P],
                 pT_ps[:, pT_bank(jt, half), :].rearrange("p (k q) -> p k q", q=P)).then_inc(done, 1)

        @block.sync
        def _(sp):
            def load_pack(h, b):
                wait_count(sp, scores_ready, TILES * (h - 1) + NQ * (b + 1))
                for l in range(2):
                    rows = slice(64 * l, 64 * l + 64)
                    sp.dma_start(raw(q_pack[rows, b, :]),
                                 q_scr[b, bass.ds(h * DH, DH), :, :].rearrange("d m t -> (d m) t")
                                 ).then_inc(pack_loaded[b], 16)
                    k_rows = k_scr[b, bass.ds(h * DH, DH), l:l + 1, :]
                    sp.dma_start(raw(k_pack[rows, b, :]), k_rows.broadcast_to([DH, 2, S])).then_inc(pack_loaded[b], 16)

            def load_v(h, b):
                wait_count(sp, pv_ready, B * (h - 1) + b + 1)
                sp.dma_start(v_sb[:, b, :, :].rearrange("p k d -> p (k d)"),
                             v_scr[b, bass.ds(h, 1), :, :].rearrange("h p n -> (h p) n")).then_inc(v_loaded[b], 16)

            def load_bias(h, qt):
                wait_count(sp, biased, TILES * (h - 1) + (B - 1) * NQ + qt + 1)
                sp.dma_start(bias_sb[:, qt, :],
                             bias[0, bass.ds(h, 1), qt * P:(qt + 1) * P, :].rearrange("h p s -> (h p) s")
                             ).then_inc(bias_loaded[qt], 16)

            def body(h):
                load_pack(h, 0)
                if isinstance(h, int) and h == 0:
                    load_bias(h, 0)
                load_pack(h, 1)
                load_v(h, 0)
                load_pack(h, 2)
                if not (isinstance(h, int) and h == 0):
                    load_bias(h, 0)
                load_bias(h, 1)
                load_v(h, 1)
                for qt in range(2, NQ):
                    load_bias(h, qt)
                load_pack(h, 3)
                load_v(h, 2)
                load_v(h, 3)

            repeat(sp, H, body)

        @block.gpsimd
        def _(pool):
            def normalise(n, i):
                wait_apart(pool, inverted, n + 1)
                pool.tensor_scalar(xs[:, i, :], xs[:, i, :], inv_sum[:, i:i + 1], 0.0, ALU.mult, ALU.add
                                   ).then_inc(normalised, 1)

            def body(h):
                for j in range(TILES):
                    n, i = TILES * h + j, j % NX
                    wait_apart(pool, biased, n + 1)
                    pool.tensor_scalar(exp_bias[:, i:i + 1], row_max[:, i:i + 1], -INV_SCALE, 0.0, ALU.mult, ALU.add
                                       ).then_inc(exp_bias_ready, 1)
                    if not (isinstance(h, int) and n < 2):
                        normalise(n - 2, (j - 2) % NX)

            repeat(pool, H, body)
            for i in (NX - 2, NX - 1):
                normalise(TILES * H - NX + i, i)

        @block.vector
        def _(dve):
            def invert(n, i):
                dve.wait_ge(exp_ready, n + 1)
                dve.reciprocal(inv_sum[:, i:i + 1], row_sum[:, i:i + 1]).then_inc(inverted, 1)

            def body(h):
                for j in range(TILES):
                    n = TILES * h + j
                    b, qt = j // NQ, j % NQ
                    if b == 0:
                        dve.wait_ge(bias_loaded[qt], 16 * (h + 1))
                    copy_half(dve, dve.tensor_copy, dve_copied, h, j, DVE_LAG, 0)
                    wait_count(dve, pT_ready, 2 * (n - NX + 1))
                    wait_apart(dve, scores_ready, n + 1)
                    dve.tensor_tensor_reduce(out=xs[:, j % NX, :], in0=scores_ps[:, j % 2, :], in1=bias_sb[:, qt, :],
                                             scale=1.0, scalar=-3.4e38, op0=ALU.add, op1=ALU.max,
                                             accum_out=row_max[:, j % NX:j % NX + 1]).then_inc(biased, 1)
                    if not (isinstance(h, int) and n < 2):
                        invert(n - 2, (j - 2) % NX)

            repeat(dve, H, body)
            for i in (NX - 2, NX - 1):
                invert(TILES * H - NX + i, i)
            for j in range(DVE_LAG):
                copy_half(dve, dve.tensor_copy, dve_copied, H, j, DVE_LAG, 0)

        @block.scalar
        def _(act):
            def copy(out, in_):
                return act.activation(out, in_, ACT.Copy)

            def take_output(group, slot):
                act.wait_ge(pv_ready, group + 1)
                wait_count(act, y_stored[slot], 32 * (group - slot))
                act.activation(y_stage[:, slot, :], y_ps[:, 0:QW], ACT.Copy).then_inc(y_taken, 1)

            def store_output(group, slot, b, h):
                act.wait_ge(y_taken, group + 1)
                for q in range(4):
                    act.dma_start(y_scr[b, q, bass.ds(h * DH, DH), :], y_stage[DH * q:DH * q + DH, slot, :]
                                  ).then_inc(y_stored[slot], 16)

            def body(h):
                for j in range(TILES):
                    n, i = TILES * h + j, j % NX
                    b, qt = j // NQ, j % NQ
                    act.wait_ge(exp_bias_ready, n + 1)
                    act.activation(xs[:, i, :], xs[:, i, :], ACT.Exp, bias=exp_bias[:, i:i + 1], scale=INV_SCALE,
                                   accum_out=row_sum[:, i:i + 1]).then_inc(exp_ready, 1)
                    copy_half(act, copy, act_copied, h, j, ACT_LAG, 1)
                    if qt in (2, 3) and not (isinstance(h, int) and h == 0 and b < 2):
                        if qt == 2:
                            take_output(B * h + b - 2, b % 2)
                        else:
                            store_output(B * h + b - 2, b % 2, (b - 2) % B, h if b >= 2 else h - 1)

            repeat(act, H, body)
            for j in range(ACT_LAG):
                copy_half(act, copy, act_copied, H, j, ACT_LAG, 1)
            for b in (B - 2, B - 1):
                take_output(B * (H - 1) + b, b % 2)
                store_output(B * (H - 1) + b, b % 2, b, H - 1)
            for slot in range(2):
                act.wait_ge(y_stored[slot], 64 * B * H // 2)

        @block.tensor
        def _(pe):
            def scores(n, j, h):
                b, qt = j // NQ, j % NQ
                if qt == 0:
                    pe.wait_ge(pack_loaded[b], 64 * (h + 1))
                wait_count(pe, biased, n - 1)
                for half in range(2):
                    last = pe.matmul(scores_ps[:, j % 2, half * TB:(half + 1) * TB],
                                     q_pack[:, b, qt * P:(qt + 1) * P], k_pack[:, b, half * TB:(half + 1) * TB],
                                     start=True, stop=True)
                last.then_inc(scores_ready, 1)

            def transposes(n, j):
                pe.wait_ge(normalised, n + 1)
                for half, copied in enumerate((dve_copied, act_copied)):
                    wait_count(pe, copied, n - 1 if half == 0 else n)
                    for k in range(4):
                        kt = 4 * half + k
                        last = pe.transpose(pT_ps[:, pT_bank(j, half), k * P:(k + 1) * P], xs[:, j % NX, kt * P:(kt + 1) * P],
                                            ident[:, :])
                    last.then_inc(pT_ready, 1)

            def outputs(group, b, kt, h):
                if kt == 0:
                    pe.wait_ge(dve_copied, NQ * (group + 1))
                    pe.wait_ge(act_copied, NQ * (group + 1))
                    pe.wait_ge(v_loaded[b], 16 * (h + 1))
                    wait_count(pe, y_taken, group)
                for q in range(4):
                    last = pe.matmul(y_ps[DH * q:DH * q + DH, 0:QW], v_sb[:, b, kt, :],
                                     probsT[:, b % 2, kt, q * QW:(q + 1) * QW],
                                     start=(kt == 0), stop=(kt == NKT - 1))
                if kt == NKT - 1:
                    last.then_inc(pv_ready, 1)

            def outputs_at(h, j):
                back = j - PV0
                if back % 2 == 0:
                    h_of = h if back >= 0 else h - 1
                    b, kt = (back % TILES) // NQ, back % NQ
                    for k in (kt, kt + 1):
                        outputs(B * h_of + b, b, k, h_of)

            def body(h):
                for j in range(TILES):
                    n = TILES * h + j
                    scores(n, j, h)
                    if not (isinstance(h, int) and n < PV0):
                        outputs_at(h, j)
                    if not (isinstance(h, int) and n < LAG):
                        transposes(n - LAG, (j - LAG) % TILES)

            repeat(pe, H, body)
            for j in range(PV0):
                if j < LAG:
                    transposes(TILES * H + j - LAG, TILES + j - LAG)
                outputs_at(H, j)


def project_out(nc, x, g_xattn, Wproj, Wr, br, y_scr, x1_scr, z2_scr, ident, experts):
    B, T, D = x.shape
    CT, HB, NE = D // P, T // TB, Wr.shape[1]
    NT = B * HB
    with ExitStack() as c:
        def sb(name, shape, dt=F32):
            return c.enter_context(nc.sbuf_tensor(name, shape, dt))

        def sem(name):
            return c.enter_context(nc.semaphore(name))

        wp_raw = sb("wp_raw", [P, CT, D])
        wp_hi, wp_lo = sb("wp_hi", [P, CT, D], F32R), sb("wp_lo", [P, CT, D], F32R)
        wr_sb = sb("wr_sb", [P, CT, NE])
        br_sb = sb("br_sb", [1, NE])
        gate, gate_t = sb("gate", [P, 1]), sb("gate_t", [P, 1])
        x_in = sb("x_in3", [P, HB, TT, D])
        y = sb("y", [P, HB, CT, TB])
        y_hi, y_lo = sb("y_hi", [P, HB, CT, TB], F32R), sb("y_lo", [P, HB, CT, TB], F32R)
        x1 = sb("x1", [P, HB, TT, D])
        z2 = sb("z2", [P, TT, D])
        zT = sb("zT", [P, HB, CT, TB])
        stats = sb("stats3", [P, TT, 6])
        moments = sb("moments3", [P, TT, 2])
        var_eps = sb("var_eps3", [P, TT])
        rstd, shift = sb("rstd3", [P, TT]), sb("shift3", [P, TT])
        minus_half = sb("minus_half3", [P, TT])
        z_sum = sb("z_sum", [P, CT, B, HB])
        z_tot = sb("z_tot", [P, CT, B])
        route = sb("route", [1, B, NE])
        best = sb("best", [1, B, 8])
        y_ps = c.enter_context(nc.psum_tensor("y_ps", [P, 4, D], F32))
        zT_ps = c.enter_context(nc.psum_tensor("zT_ps3", [P, 2, TB], F32))
        route_ps = c.enter_context(nc.psum_tensor("route_ps", [1, B, NE], F32))

        wp_loaded, small_loaded = sem("wp_loaded"), sem("small_loaded")
        y_loaded = [sem(f"y_loaded{u}") for u in range(HB)]
        x_loaded = [sem(f"x_loaded3{u}") for u in range(HB)]
        wp_hi_ready, wp_ready, gate_ready, const_ready = sem("wp_hi_ready"), sem("wp_ready"), sem("gate_ready"), sem("const3")
        y_hi_ready, y_lo_ready, y_done = sem("y_hi_ready"), sem("y_lo_ready"), sem("y_done")
        y_lo_first = sem("y_lo_first")
        x1_ready, stats_ready, moments_ready, eps_added = sem("x1_ready"), sem("stats_ready3"), sem("moments3s"), sem("eps3")
        rstd_ready, z_ready, zT_ready = sem("rstd3s"), sem("z_ready3"), sem("zT_ready3")
        shift_ready, zT_taken = sem("shift_ready"), sem("zT_taken")
        x1_stored = [sem(f"x1_stored{u}") for u in range(HB)]
        z_stored = [sem(f"z_stored{u}") for u in range(HB)]
        tot_ready, route_done, route_ready, best_ready, expert_ready = (
            sem("tot_ready"), sem("route_done"), sem("route_ready"), sem("best_ready"), sem("expert_ready"))
        block = c.enter_context(nc.Block())

        @block.sync
        def _(sp):
            sp.dma_start(wp_raw[:, :, :], Wproj.rearrange("(c p) n -> p c n", p=P)).then_inc(wp_loaded, 16)
            sp.dma_start(wr_sb[:, :, :], Wr.rearrange("(c p) e -> p c e", p=P)).then_inc(small_loaded, 16)
            sp.dma_start(br_sb[:, :], br.rearrange("(a e) -> a e", a=1)).then_inc(small_loaded, 16)
            sp.dma_start(gate[:, :], g_xattn.rearrange("(a e) -> a e", a=1).broadcast_to([P, 1])).then_inc(small_loaded, 16)

            def loads(b):
                for u in range(HB):
                    t = HB * b + u
                    if not (isinstance(b, int) and b == 0):
                        sp.wait_ge(y_lo_first, 1)
                        sp.wait_ge(y_lo_ready, t - 1 - u)
                    for q in range(2):
                        sp.dma_start(y[:, u, :, q * (TB // 2):(q + 1) * (TB // 2)],
                                     y_scr[b, 2 * u + q, :, :].rearrange("(c p) t -> p c t", p=P)
                                     ).then_inc(y_loaded[u], 16)
                    wait_count(sp, x1_ready, TT * (t - 1))
                    sp.dma_start(x_in[:, u, :, :], x[b, u * TB:(u + 1) * TB, :].rearrange("(j p) n -> p j n", p=P)
                                 ).then_inc(x_loaded[u], 16)

            repeat(sp, B, loads)
            for u in range(HB):
                sp.wait_ge(x1_stored[u], 16 * B)
                sp.wait_ge(z_stored[u], 16 * B)

        @block.gpsimd
        def _(pool):
            pool.memset(minus_half[:, :], -0.5).then_inc(const_ready, 1)
            pool.wait_ge(const_ready, 1)

            def y_lo_of(t, u):
                pool.wait_ge(y_hi_ready, t + 1)
                pool.tensor_tensor(y_lo[:, u, :, :], y[:, u, :, :], raw(y_hi[:, u, :, :]), ALU.subtract
                                   ).then_inc(y_lo_ready, 1)

            y_lo_of(1, 1)

            def body(b):
                for u in range(HB):
                    t = HB * b + u
                    pool.wait_ge(eps_added, t + 1)
                    pool.tensor_tensor(rstd[:, :], var_eps[:, :], minus_half[:, :], ALU.pow).then_inc(rstd_ready, 1)
                    pool.wait_ge(rstd_ready, t + 1)
                    pool.tensor_tensor(shift[:, :], moments[:, :, 0], rstd[:, :], ALU.mult).then_inc(shift_ready, 1)
                    wait_apart(pool, shift_ready, 2 * t + 1)
                    pool.tensor_scalar(shift[:, :], shift[:, :], -1.0, 0.0, ALU.mult, ALU.add).then_inc(shift_ready, 1)
                    wait_count(pool, zT_ready, CT * t)
                    wait_apart(pool, shift_ready, 2 * t + 2)
                    for j in range(TT):
                        last = pool.tensor_scalar(z2[:, j, :], x1[:, u, j, :], rstd[:, j:j + 1], shift[:, j:j + 1],
                                                  ALU.mult, ALU.add)
                    last.then_inc(z_ready, 1)
                    if not is_last(b, B):
                        y_lo_of(t + 2, u)

            repeat(pool, B, body)

        @block.scalar
        def _(act):
            act.wait_ge(small_loaded, 48)
            act.activation(gate_t[:, :], gate[:, :], ACT.Tanh).then_inc(gate_ready, 1)

            def y_hi_of(t, b, u):
                act.wait_ge(y_loaded[u], 32 * (b + 1))
                wait_count(act, y_done, TT * (t - 1))
                act.activation(y_hi[:, u, :, :], y[:, u, :, :], ACT.Copy).then_inc(y_hi_ready, 1)

            y_hi_of(0, 0, 0)
            y_hi_of(1, 0, 1)

            def body(b):
                for u in range(HB):
                    t = HB * b + u
                    act.wait_ge(x1_ready, TT * (t + 1))
                    act.dma_start(x1_scr[bass.ds(t * TB, TB), :].rearrange("(j p) n -> p j n", p=P), x1[:, u, :, :]
                                  ).then_inc(x1_stored[u], 16)
                    if not is_last(b, B):
                        y_hi_of(t + 2, b + 1, u)
                    wait_count(act, z_stored[u], 16 * b)
                    for ct in range(CT):
                        act.wait_ge(zT_ready, CT * t + ct + 1)
                        act.activation(zT[:, u, ct, :], zT_ps[:, ct % 2, :], ACT.Copy,
                                       accum_out=z_sum[:, ct, b, u:u + 1] if isinstance(b, int)
                                       else z_sum[:, ct, bass.ds(b, 1), u]).then_inc(zT_taken, 1)
                    act.wait_ge(zT_taken, CT * (t + 1))
                    act.dma_start(z2_scr[bass.ds(t, 1), :, :, :].rearrange("a p c t -> (a p) c t"), zT[:, u, :, :]
                                  ).then_inc(z_stored[u], 16)

            repeat(act, B, body)

        @block.vector
        def _(dve):
            dve.wait_ge(wp_loaded, 16)
            dve.tensor_copy(wp_hi[:, :, :], wp_raw[:, :, :]).then_inc(wp_hi_ready, 1)
            dve.wait_ge(wp_hi_ready, 1)
            dve.tensor_tensor(wp_lo[:, :, :], wp_raw[:, :, :], raw(wp_hi[:, :, :]), ALU.subtract).then_inc(wp_ready, 1)

            dve.wait_ge(y_hi_ready, 1)
            dve.tensor_tensor(y_lo[:, 0, :, :], y[:, 0, :, :], raw(y_hi[:, 0, :, :]), ALU.subtract).then_inc(y_lo_first, 1)
            dve.wait_ge(gate_ready, 1)

            def body(b):
                for u in range(HB):
                    t = HB * b + u
                    dve.wait_ge(x_loaded[u], 16 * (b + 1))
                    wait_count(dve, x1_stored[u], 16 * b)
                    wait_count(dve, z_ready, t - 1)
                    for j in range(TT):
                        dve.wait_ge(y_done, TT * t + j + 1)
                        dve.scalar_tensor_tensor(x1[:, u, j, :], y_ps[:, j, :], gate_t[:, 0:1], x_in[:, u, j, :],
                                                 ALU.mult, ALU.add).then_inc(x1_ready, 1)
                        if j:
                            dve.wait_ge(x1_ready, TT * t + j)
                            dve.bn_stats(stats[:, j - 1, :], x1[:, u, j - 1, :]).then_inc(stats_ready, 1)
                    dve.wait_ge(x1_ready, TT * (t + 1))
                    dve.bn_stats(stats[:, TT - 1, :], x1[:, u, TT - 1, :]).then_inc(stats_ready, 1)
                    wait_apart(dve, stats_ready, TT * (t + 1))
                    if not (isinstance(t, int) and t == 0):
                        wait_apart(dve, shift_ready, 2 * t - 1)
                    for j in range(TT):
                        last = dve.bn_aggr(moments[:, j, :], stats[:, j, :])
                    last.then_inc(moments_ready, 1)
                    dve.wait_ge(moments_ready, t + 1)
                    wait_count(dve, rstd_ready, t)
                    dve.tensor_scalar(var_eps[:, :], moments[:, :, 1], EPS, None, ALU.add).then_inc(eps_added, 1)

            repeat(dve, B, body)
            dve.wait_ge(zT_taken, CT * NT)
            dve.tensor_tensor(z_tot[:, :, :], z_sum[:, :, :, 0], z_sum[:, :, :, 1], ALU.add).then_inc(tot_ready, 1)
            dve.wait_ge(route_done, 1)
            dve.wait_ge(small_loaded, 48)
            for b in range(B):
                last = dve.scalar_tensor_tensor(route[:, b, :], route_ps[:, b, :], 1.0 / T, br_sb[:, :],
                                                ALU.mult, ALU.add)
            last.then_inc(route_ready, 1)
            dve.wait_ge(route_ready, 1)
            for b in range(B):
                last = dve.max(best[:, b, :], route[:, b, :])
            last.then_inc(best_ready, 1)
            dve.wait_ge(best_ready, 1)
            for b in range(B):
                last = dve.max_index(experts[:, b, :], best[:, b, :], route[:, b, :])
            last.then_inc(expert_ready, 1)

        @block.tensor
        def _(pe):
            def product(t, u, j):
                wait_count(pe, x1_ready, TT * (t - 1) + j + 1)
                for ct in range(CT):
                    for n, (a, w) in enumerate(((y_hi, wp_hi), (y_hi, wp_lo), (y_lo, wp_hi))):
                        last = pe.matmul(y_ps[:, j, :], a[:, u, ct, j * P:(j + 1) * P], w[:, ct, :],
                                         start=(ct == 0 and n == 0), stop=(ct == CT - 1 and n == 2))
                last.then_inc(y_done, 1)

            def transposes(t, ct):
                wait_count(pe, zT_taken, CT * t + ct - 1)
                for j in range(TT):
                    last = pe.transpose(zT_ps[:, ct % 2, j * P:(j + 1) * P], z2[:, j, ct * P:(ct + 1) * P], ident[:, :])
                last.then_inc(zT_ready, 1)

            pe.wait_ge(wp_ready, 1)
            pe.wait_ge(y_lo_first, 1)
            for j in range(TT):
                product(0, 0, j)

            def body(b):
                for u in range(HB):
                    t = HB * b + u
                    more = not (is_last(b, B) and u == HB - 1)
                    if more:
                        pe.wait_ge(y_lo_ready, t + 1)
                        for j in range(TT - 1):
                            product(t + 1, (u + 1) % HB, j)
                    pe.wait_ge(z_ready, t + 1)
                    transposes(t, 0)
                    transposes(t, 1)
                    if more:
                        product(t + 1, (u + 1) % HB, TT - 1)
                    transposes(t, 2)
                    transposes(t, 3)

            repeat(pe, B, body)
            pe.wait_ge(tot_ready, 1)
            pe.wait_ge(small_loaded, 48)
            for b in range(B):
                for ct in range(CT):
                    last = pe.matmul(route_ps[:, b, :], z_tot[:, ct, b:b + 1], wr_sb[:, ct, :],
                                     start=(ct == 0), stop=(ct == CT - 1))
            last.then_inc(route_done, 1)


def expert_ffn(nc, g_ffn, W1c, b1c, W2, b2, x1_scr, z2_scr, experts, out, B, T):
    NE, NF, _, D = W1c.shape
    CT, HB = D // P, T // TB
    NW = 4
    with ExitStack() as c:
        def sb(name, shape, dt=F32):
            return c.enter_context(nc.sbuf_tensor(name, shape, dt))

        def sem(name):
            return c.enter_context(nc.semaphore(name))

        w_raw = sb("w_raw", [P, NW, 2, D])
        w_hi, w_lo = sb("w_hi", [P, NW, 2, D], F32R), sb("w_lo", [P, NW, 2, D], F32R)
        z_in = sb("z_in", [P, CT, TB])
        zT = sb("zT4", [P, HB, 2, CT, TB], F32R)
        h_full = sb("h_full", [P, 2, TB])
        h_hi, h_lo = sb("h_hi", [P, 2, TB], F32R), sb("h_lo", [P, 2, TB], F32R)
        x1 = sb("x14", [P, HB, TT, D])
        b1_sb = sb("b1_sb", [P, B, NF])
        b2_sb = sb("b2_sb", [P, B, D])
        b2_gated = sb("b2_gated", [P, D])
        gate, gate_t = sb("gate4", [P, 1]), sb("gate_t4", [P, 1])
        h_ps = c.enter_context(nc.psum_tensor("h_ps", [P, 2, TB], F32))
        y_ps = c.enter_context(nc.psum_tensor("y_ps4", [P, TT, D], F32))

        w_loaded = [sem(f"w_loaded{i}") for i in range(NW)]
        z_loaded, z_hi_ready, z_lo_ready = sem("z_loaded"), sem("z_hi_ready4"), sem("z_lo_ready4")
        x1_loaded = [sem(f"x1_loaded{u}") for u in range(HB)]
        b_loaded = sem("b_loaded")
        gate_loaded, gate_ready, b2_ready, x1_biased = sem("gate_loaded"), sem("gate_ready4"), sem("b2_ready"), sem("x1_biased")
        w_hi_ready, w_lo_ready = sem("w_hi4"), sem("w_lo4")
        hT_ready, h_full_ready, h_hi_ready, h_lo_ready = sem("hT_ready"), sem("h_full_ready"), sem("h_hi4"), sem("h_lo4")
        chunk_done, y_done, res_ready = sem("chunk_done"), sem("y_done4"), sem("res_ready")
        out_stored = [sem(f"out_stored{u}") for u in range(HB)]
        block = c.enter_context(nc.Block())

        @block.sync
        def _(sp):
            sp.dma_start(gate[:, :], g_ffn.rearrange("(a e) -> a e", a=1).broadcast_to([P, 1])).then_inc(gate_loaded, 16)

            def load_z(t):
                wait_count(sp, z_lo_ready, t)
                sp.dma_start(z_in[:, :, :], z2_scr[bass.ds(t, 1), :, :, :].rearrange("a p c t -> (a p) c t")
                             ).then_inc(z_loaded, 16)

            load_z(0)

            def body(b):
                e = sp.value_load(experts[0:1, bass.ds(b, 1), 0:1].rearrange("p a e -> p (a e)"), min_val=0, max_val=NE - 1)
                sp.dma_start(b1_sb[:, bass.ds(b, 1), :], b1c[bass.ds(e, 1), :, :].rearrange("a p f -> p a f")
                             ).then_inc(b_loaded, 16)
                sp.dma_start(b2_sb[:, bass.ds(b, 1), :], b2[bass.ds(e, 1), :].rearrange("(c a) n -> c a n", c=1
                                                                                       ).broadcast_to([P, 1, D])
                             ).then_inc(b_loaded, 16)
                sp.wait_ge(b_loaded, 32 * (b + 1))
                for u in range(HB):
                    t = HB * b + u
                    for f in range(NF):
                        slot = f % NW
                        wait_count(sp, w_lo_ready, NF * t + f - NW + 1)
                        sp.dma_start(w_raw[:, slot, 0, :], W1c[bass.ds(e, 1), f, :, :].rearrange("a p n -> (a p) n")
                                     ).then_inc(w_loaded[slot], 16)
                        sp.dma_start(w_raw[:, slot, 1, :], W2[bass.ds(e, 1), f * P:(f + 1) * P, :
                                                             ].rearrange("a p n -> (a p) n")
                                     ).then_inc(w_loaded[slot], 16)
                        if f == NW and not (is_last(b, B) and u == HB - 1):
                            load_z(t + 1)
                        if f == NW:
                            wait_count(sp, out_stored[u], 16 * b)
                            sp.dma_start(x1[:, u, :, :], x1_scr[bass.ds(t * TB, TB), :
                                                               ].rearrange("(j p) n -> p j n", p=P)
                                         ).then_inc(x1_loaded[u], 16)

            repeat(sp, B, body)

        @block.gpsimd
        def _(pool):
            pool.wait_ge(gate_ready, 1)

            def body(b):
                pool.wait_ge(b_loaded, 32 * (b + 1))
                wait_count(pool, x1_biased, HB * b)
                pool.tensor_tensor(b2_gated[:, :], b2_sb[:, bass.ds(b, 1), :].rearrange("p a n -> p (a n)"),
                                   gate_t[:, 0:1].broadcast_to([P, D]), ALU.mult).then_inc(b2_ready, 1)
                pool.wait_ge(b2_ready, b + 1)
                for u in range(HB):
                    t = HB * b + u
                    pool.wait_ge(x1_loaded[u], 16 * (b + 1))
                    for j in range(TT):
                        last = pool.tensor_tensor(x1[:, u, j, :], x1[:, u, j, :], b2_gated[:, :], ALU.add)
                    last.then_inc(x1_biased, 1)

            repeat(pool, B, body)

        @block.scalar
        def _(act):
            act.wait_ge(gate_loaded, 16)
            act.activation(gate_t[:, :], gate[:, :], ACT.Tanh).then_inc(gate_ready, 1)

            def split_z(t, u):
                act.wait_ge(z_loaded, 16 * (t + 1))
                wait_count(act, chunk_done, NF * (t - 1))
                act.activation(zT[:, u, 0, :, :], z_in[:, :, :], ACT.Copy).then_inc(z_hi_ready, 1)

            split_z(0, 0)

            def store(t, u):
                act.wait_ge(res_ready, TT * (t + 1))
                act.dma_start(out[bass.ds(t * TB, TB), :].rearrange("(j p) n -> p j n", p=P), x1[:, u, :, :]
                              ).then_inc(out_stored[u], 16)

            def body(b):
                act.wait_ge(b_loaded, 32 * (b + 1))
                for u in range(HB):
                    t = HB * b + u
                    for f in range(NF):
                        n = NF * t + f
                        b1 = b1_sb[:, bass.ds(b, 1), f:f + 1].rearrange("p a f -> p (a f)")
                        wait_count(act, h_lo_ready, n - 1)
                        wait_apart(act, hT_ready, n + 1)
                        act.activation(h_full[:, f % 2, :], h_ps[:, f % 2, :], ACT.Relu, bias=b1
                                       ).then_inc(h_full_ready, 1)
                        if not (isinstance(n, int) and n < 2):
                            wait_apart(act, chunk_done, n - 1)
                        act.activation(h_hi[:, f % 2, :], h_ps[:, f % 2, :], ACT.Relu, bias=b1).then_inc(h_hi_ready, 1)
                        if f == 2 and not (isinstance(t, int) and t == 0):
                            store(t - 1, (u + 1) % HB)
                        if f == NF // 2 and not (is_last(b, B) and u == HB - 1):
                            split_z(t + 1, (u + 1) % HB)

            repeat(act, B, body)
            store(B * HB - 1, HB - 1)
            for u in range(HB):
                act.wait_ge(out_stored[u], 16 * B)

        @block.vector
        def _(dve):
            def split_chunk(n, f, count):
                slot = f % NW
                dve.wait_ge(w_loaded[slot], 32 * count)
                wait_count(dve, chunk_done, n - NW + 1)
                dve.tensor_copy(w_hi[:, slot, :, :], w_raw[:, slot, :, :]).then_inc(w_hi_ready, 1)
                dve.wait_ge(w_hi_ready, n + 1)
                dve.tensor_tensor(w_lo[:, slot, :, :], w_raw[:, slot, :, :], raw(w_hi[:, slot, :, :]), ALU.subtract
                                  ).then_inc(w_lo_ready, 1)

            def split_z(t, u):
                dve.wait_ge(z_hi_ready, t + 1)
                dve.tensor_tensor(zT[:, u, 1, :, :], z_in[:, :, :], raw(zT[:, u, 0, :, :]), ALU.subtract
                                  ).then_inc(z_lo_ready, 1)

            split_z(0, 0)
            split_chunk(0, 0, 1)
            split_chunk(1, 1, 1)

            def body(b):
                for u in range(HB):
                    t = HB * b + u
                    for f in range(NF):
                        n = NF * t + f
                        dve.wait_ge(h_hi_ready, n + 1)
                        dve.tensor_tensor(h_lo[:, f % 2, :], h_full[:, f % 2, :], raw(h_hi[:, f % 2, :]), ALU.subtract
                                          ).then_inc(h_lo_ready, 1)
                        if not (is_last(b, B) and u == HB - 1 and f >= NF - 2):
                            f2 = (f + 2) % NF
                            split_chunk(n + 2, f2, (NF // NW) * (t + (f + 2) // NF) + f2 // NW + 1)
                        if f == NF // 2 + 1 and not (is_last(b, B) and u == HB - 1):
                            split_z(t + 1, (u + 1) % HB)
                    dve.wait_ge(x1_biased, t + 1)
                    for j in range(TT):
                        if j < TT - 1:
                            dve.wait_ge(y_done, (TT - 1) * t + j + 1)
                        else:
                            dve.wait_ge(chunk_done, NF * (t + 1))
                        dve.scalar_tensor_tensor(x1[:, u, j, :], y_ps[:, j, :], gate_t[:, 0:1], x1[:, u, j, :],
                                                 ALU.mult, ALU.add).then_inc(res_ready, 1)

            dve.wait_ge(gate_ready, 1)
            repeat(dve, B, body)

        @block.tensor
        def _(pe):
            def hidden(t, b, u, f):
                n = NF * t + f
                if f == 0:
                    pe.wait_ge(z_lo_ready, t + 1)
                pe.wait_ge(w_lo_ready, n + 1)
                wait_count(pe, h_hi_ready, n - 1)
                for ct in range(CT):
                    cs = slice(ct * P, (ct + 1) * P)
                    for i, (w, l) in enumerate(((w_hi, 0), (w_hi, 1), (w_lo, 0))):
                        last = pe.matmul(h_ps[:, f % 2, :], w[:, f % NW, 0, cs], zT[:, u, l, ct, :],
                                         start=(ct == 0 and i == 0), stop=(ct == CT - 1 and i == 2))
                last.then_inc(hT_ready, 1)

            def result(t, f):
                n = NF * t + f
                pe.wait_ge(h_lo_ready, n + 1)
                for j in range(TT):
                    if f == 0:
                        wait_count(pe, res_ready, TT * (t - 1) + j + 1)
                    js = slice(j * P, (j + 1) * P)
                    for i, (a, w) in enumerate(((h_hi, w_hi), (h_hi, w_lo), (h_lo, w_hi))):
                        last = pe.matmul(y_ps[:, j, :], a[:, f % 2, js], w[:, f % NW, 1, :],
                                         start=(f == 0 and i == 0), stop=(f == NF - 1 and i == 2))
                    if f == NF - 1 and j < TT - 1:
                        last.then_inc(y_done, 1)
                last.then_inc(chunk_done, 1)

            hidden(0, 0, 0, 0)

            def body(b):
                for u in range(HB):
                    t = HB * b + u
                    for f in range(NF):
                        if f < NF - 1:
                            hidden(t, b, u, f + 1)
                        elif not (is_last(b, B) and u == HB - 1):
                            hidden(t + 1, b + (u + 1) // HB, (u + 1) % HB, 0)
                        result(t, f)

            repeat(pe, B, body)



def kernel(x, ctx_1024, g_xattn, g_ffn, L0_xattn_position_bias, L0_xattn_W_q, L0_xattn_W_kv, L0_xattn_W_proj,
           L0_ffn_Wr, L0_ffn_br, L0_ffn_W1, L0_ffn_b1, L0_ffn_W2, L0_ffn_b2):
    import numpy as np
    import concourse.bacc as bacc
    from concourse import mybir as mb
    from concourse.bass_utils import run_bass_kernel_spmd

    W1, b1 = np.asarray(L0_ffn_W1), np.asarray(L0_ffn_b1)
    E, D, F = W1.shape
    arrays = {
        "x": x,
        "ctxT": np.asarray(ctx_1024).transpose(0, 2, 1),
        "g_xattn": g_xattn,
        "g_ffn": g_ffn,
        "bias": L0_xattn_position_bias,
        "Wq": L0_xattn_W_q,
        "Wkv": L0_xattn_W_kv,
        "Wproj": L0_xattn_W_proj,
        "Wr": L0_ffn_Wr,
        "br": L0_ffn_br,
        "W1c": W1.reshape(E, D // 128, 128, F // 128, 128).transpose(0, 3, 2, 1, 4).reshape(E, F // 128, 128, D),
        "b1c": b1.reshape(E, F // 128, 128).transpose(0, 2, 1),
        "W2": L0_ffn_W2,
        "b2": L0_ffn_b2,
    }
    arrays = {k: np.ascontiguousarray(v) for k, v in arrays.items()}
    nc = bacc.Bacc("TRN2", target_bir_lowering=False, num_devices=1)
    ins = [nc.dram_tensor(k, v.shape, mb.dt.from_np(v.dtype), kind="ExternalInput").ap() for k, v in arrays.items()]
    shape = tuple(np.asarray(x).shape)
    out = nc.dram_tensor("out", (shape[0] * shape[1], shape[2]), mb.dt.float32, kind="ExternalOutput").ap()
    gated_block(nc, *ins, out)
    r = run_bass_kernel_spmd(nc, [arrays], core_ids=[0])
    return r.results[0]["out"].reshape(shape)
```

```python
import concourse.bass as bass
from concourse import mybir
from contextlib import ExitStack

F32 = mybir.dt.float32
F32R = mybir.dt.float32r
U32 = mybir.dt.uint32
ALU = mybir.AluOpType
ACT = mybir.ActivationFunctionType

P = 128
TB = 512
TT = TB // P
EPS = 1e-5


def wait_count(eng, sem, n):
    if not (isinstance(n, int) and n <= 0):
        eng.wait_ge(sem, n)


def wait_apart(eng, sem, n):
    if isinstance(n, int):
        eng.wait_ge(sem, n)
    else:
        count = eng.to_reg(n)
        eng.wait_ge(sem, 1)
        eng.wait_ge(sem, count)


def repeat(eng, n, body):
    body(0)
    with eng.Fori(1, n - 1) as i:
        body(i)
    body(n - 1)


def is_last(i, n):
    return isinstance(i, int) and i == n - 1


def raw(ap):
    return ap.bitcast(F32)


def gated_block(nc, x, ctxT, g_xattn, g_ffn, bias, Wq, Wkv, Wproj, Wr, br, W1c, b1c, W2, b2, out):
    B, T, D = x.shape
    H = bias.shape[1]
    DH = D // H
    S = ctxT.shape[2]
    NE, NF, _, CTF = W1c.shape
    CT = D // P
    HB = T // TB
    NQ = T // P
    NKT = S // P
    INV_SCALE = float(DH) ** 0.5
    assert (D, DH, T, S, HB, CTF) == (CT * P, 32, NQ * P, T, 2, CT * P)

    q_scr = nc.dram_tensor("q_scr", (B, D, 2, T), F32, kind="Internal").ap()
    k_scr = nc.dram_tensor("k_scr", (B, D, 2, S), F32, kind="Internal").ap()
    v_scr = nc.dram_tensor("v_scr", (B, H, P, NKT * DH), F32, kind="Internal").ap()
    y_scr = nc.dram_tensor("y_scr", (B, 4, D, T // 4), F32, kind="Internal").ap()
    x1_scr = nc.dram_tensor("x1_scr", (B * T, D), F32, kind="Internal").ap()
    z2_scr = nc.dram_tensor("z2_scr", (B * HB, P, CT, TB), F32, kind="Internal").ap()

    with ExitStack() as top:
        ident = top.enter_context(nc.sbuf_tensor("ident", [P, P], F32))
        experts = top.enter_context(nc.sbuf_tensor("experts", [1, B, 8], U32))
        project_qkv(nc, x, ctxT, Wq, Wkv, q_scr, k_scr, v_scr, ident)
        proj = ProjectionInputs(nc, top, CT, HB, T)
        attention(nc, bias, Wproj, q_scr, k_scr, v_scr, y_scr, ident, proj, B, T, S, H, DH, INV_SCALE)
        ffn = FfnInputs(nc, top, CT, HB)
        project_out(nc, x, g_xattn, Wr, br, y_scr, x1_scr, z2_scr, ident, experts, proj, ffn)
        expert_ffn(nc, g_ffn, W1c, b1c, W2, b2, x1_scr, z2_scr, experts, out, ffn, B, T)


class ProjectionInputs:

    def __init__(self, nc, stack, CT, HB, T):
        def sb(name, shape, dt=F32):
            return stack.enter_context(nc.sbuf_tensor(name, shape, dt))

        def sem(name):
            return stack.enter_context(nc.semaphore(name))

        self.wp_raw = sb("wp_raw", [P, CT, CT * P])
        self.wp_hi, self.wp_lo = sb("wp_hi", [P, CT, CT * P], F32R), sb("wp_lo", [P, CT, CT * P], F32R)
        self.y = sb("y", [P, HB, CT, TB])
        self.y_stage = sb("y_stage", [P, 2, T // 4])
        self.wp_loaded, self.wp_hi_ready, self.wp_ready = sem("wp_loaded"), sem("wp_hi_ready"), sem("wp_ready")
        self.y_loaded = [sem(f"y_loaded{u}") for u in range(HB)]
        self.y_stored = [sem(f"y_stored{i}") for i in range(2)]


class FfnInputs:

    def __init__(self, nc, stack, CT, HB):
        def sem(name):
            return stack.enter_context(nc.semaphore(name))

        self.z_in = stack.enter_context(nc.sbuf_tensor("z_in", [P, CT, TB], F32))
        self.zT = stack.enter_context(nc.sbuf_tensor("zT4", [P, HB, 2, CT, TB], F32R))
        self.x1 = stack.enter_context(nc.sbuf_tensor("x1", [P, HB, TB // P, CT * P], F32))
        self.z2T = stack.enter_context(nc.sbuf_tensor("z2T", [P, HB, CT, TB], F32))
        self.z_loaded, self.z_hi_ready, self.z_lo_ready = sem("z_loaded"), sem("z_hi_ready"), sem("z_lo_ready")
        self.x1_stored = [sem(f"x1_stored{u}") for u in range(HB)]
        self.z_stored = [sem(f"z_stored{u}") for u in range(HB)]

    def load(self, sp, z2_scr, t):
        sp.dma_start(self.z_in[:, :, :], z2_scr[bass.ds(t, 1), :, :, :].rearrange("a p c t -> (a p) c t")
                     ).then_inc(self.z_loaded, 16)

    def split_hi(self, act, t, u):
        act.wait_ge(self.z_loaded, 16 * (t + 1))
        act.activation(self.zT[:, u, 0, :, :], self.z_in[:, :, :], ACT.Copy).then_inc(self.z_hi_ready, 1)

    def split_lo(self, dve, t, u):
        dve.wait_ge(self.z_hi_ready, t + 1)
        dve.tensor_tensor(self.zT[:, u, 1, :, :], self.z_in[:, :, :], raw(self.zT[:, u, 0, :, :]), ALU.subtract
                          ).then_inc(self.z_lo_ready, 1)


def project_qkv(nc, x, ctxT, Wq, Wkv, q_scr, k_scr, v_scr, ident):
    B, T, D = x.shape
    CT, HB, DH = D // P, T // TB, 32
    H = D // DH
    OUTS = 3 * CT
    with ExitStack() as c:
        def sb(name, shape, dt=F32):
            return c.enter_context(nc.sbuf_tensor(name, shape, dt))

        def sem(name):
            return c.enter_context(nc.semaphore(name))

        wq_raw = sb("wq_raw", [P, CT, D])
        wkv_raw = sb("wkv_raw", [P, CT, 2 * D])
        wq_hi, wq_lo = sb("wq_hi", [P, CT, D], F32R), sb("wq_lo", [P, CT, D], F32R)
        wkv_hi, wkv_lo = sb("wkv_hi", [P, CT, 2 * D], F32R), sb("wkv_lo", [P, CT, 2 * D], F32R)
        xin = sb("xin", [P, HB, TT, D])
        cin = sb("cin", [P, HB, CT, TB])
        c_hi, c_lo = sb("c_hi", [P, CT, TB], F32R), sb("c_lo", [P, CT, TB], F32R)
        z = sb("z", [P, TT, D])
        z_hi, z_lo = sb("z_hi", [P, CT, TB], F32R), sb("z_lo", [P, CT, TB], F32R)
        qk_out = sb("qk_out", [P, 4, 2, TB], F32R)
        v_out = sb("v_out", [P, H, HB * TT, DH])
        stats = sb("stats", [P, TT, 6])
        moments = sb("moments", [P, TT, 2])
        var_eps = sb("var_eps", [P, TT])
        rstd = sb("rstd", [P, TT])
        minus_half = sb("minus_half", [P, TT])
        zT_ps = c.enter_context(nc.psum_tensor("zT_ps", [P, 2, TB], F32))
        out_ps = c.enter_context(nc.psum_tensor("out_ps", [P, 4, TB], F32))

        wk_loaded, wv_loaded, wq_loaded = sem("wk_loaded"), sem("wv_loaded"), sem("wq_loaded")
        x_loaded = [sem(f"x_loaded{u}") for u in range(HB)]
        c_loaded = [sem(f"c_loaded{u}") for u in range(HB)]
        w_hi_ready, w_lo_ready = sem("w_hi_ready"), sem("w_lo_ready")
        ident_ready, const_ready = sem("ident_ready"), sem("const_ready")
        c_hi_ready, c_lo_ready = sem("c_hi_ready"), sem("c_lo_ready")
        c_lo_first = sem("c_lo_first")
        stats_ready, moments_ready, rstd_ready = sem("stats_ready"), sem("moments_ready"), sem("rstd_ready")
        eps_added = sem("eps_added")
        z_ready, zT_ready, z_hi_ready, z_lo_ready = sem("z_ready"), sem("zT_ready"), sem("z_hi_ready"), sem("z_lo_ready")
        out_ready = sem("out_ready")
        act_out, dve_out = sem("act_out"), sem("dve_out")
        qk_stored = [sem(f"qk_stored{i}") for i in range(4)]
        v_stored = sem("v_stored")

        block = c.enter_context(nc.Block())

        @block.sync
        def _(sp):
            W = Wkv.rearrange("(c p) n -> p c n", p=P)
            sp.dma_start(wkv_raw[:, :, 0:D], W[:, :, 0:D]).then_inc(wk_loaded, 16)

            def loads(b):
                for u in range(HB):
                    t = HB * b + u
                    if not (isinstance(b, int) and b == 0):
                        sp.wait_ge(c_lo_first, 1)
                        sp.wait_ge(c_lo_ready, t - 1)
                    sp.dma_start(cin[:, u, :, :], ctxT[b, :, u * TB:(u + 1) * TB].rearrange("(c p) t -> p c t", p=P)
                                 ).then_inc(c_loaded[u], 16)
                    if isinstance(b, int) and t == 0:
                        sp.dma_start(wkv_raw[:, :, D:2 * D], W[:, :, D:2 * D]).then_inc(wv_loaded, 16)
                    wait_count(sp, z_ready, t - 1)
                    sp.dma_start(xin[:, u, :, :], x[b, u * TB:(u + 1) * TB, :].rearrange("(j p) n -> p j n", p=P)
                                 ).then_inc(x_loaded[u], 16)
                    if isinstance(b, int) and t == 0:
                        sp.dma_start(wq_raw[:, :, :], Wq.rearrange("(c p) n -> p c n", p=P)).then_inc(wq_loaded, 16)

            repeat(sp, B, loads)

        @block.gpsimd
        def _(pool):
            pool.memset(ident[:, :], 0.0).then_inc(ident_ready, 1)
            pool.memset(minus_half[:, :], -0.5).then_inc(const_ready, 1)
            pool.wait_ge(ident_ready, 1)
            pool.affine_select(out=ident[:, :], in_=ident[:, :], compare_op=ALU.not_equal, fill=1.0,
                               base=0, pattern=[[-1, P]], channel_multiplier=1).then_inc(ident_ready, 1)
            pool.wait_ge(const_ready, 1)

            def body(b):
                for u in range(HB):
                    t = HB * b + u
                    pool.wait_ge(c_hi_ready, t + 1)
                    cts = slice(CT // 2, CT) if isinstance(b, int) and t == 0 else slice(0, CT)
                    pool.tensor_tensor(c_lo[:, cts, :], cin[:, u, cts, :], raw(c_hi[:, cts, :]), ALU.subtract
                                       ).then_inc(c_lo_ready, 1)
                    pool.wait_ge(eps_added, t + 1)
                    wait_count(pool, z_ready, t)
                    pool.tensor_tensor(rstd[:, :], var_eps[:, :], minus_half[:, :], ALU.pow).then_inc(rstd_ready, 1)

            repeat(pool, B, body)

        @block.scalar
        def _(act):
            def take_hi(t, i, s):
                slot = s % 4
                wait_count(act, qk_stored[slot], 16 * (2 * t + s // 4))
                act.wait_ge(out_ready, OUTS * t + i + 1)
                act.activation(qk_out[:, slot, 0, :], out_ps[:, i % 4, :], ACT.Copy).then_inc(act_out, 1)

            def store(scr, t, b, u, ct, s):
                slot = s % 4
                act.wait_ge(dve_out, 2 * CT * t + s + 1)
                act.dma_start(scr[b, ct * P:(ct + 1) * P, :, u * TB:(u + 1) * TB], raw(qk_out[:, slot, :, :])
                              ).then_inc(qk_stored[slot], 16)

            def body(b):
                for u in range(HB):
                    t = HB * b + u
                    for i in range(CT):
                        take_hi(t, i, i)
                        if i:
                            store(k_scr, t, b, u, i - 1, i - 1)
                    for ct in range(CT):
                        act.wait_ge(zT_ready, CT * t + ct + 1)
                        act.activation(z_hi[:, ct, :], zT_ps[:, ct % 2, :], ACT.Copy).then_inc(z_hi_ready, 1)
                        if ct == 0:
                            store(k_scr, t, b, u, CT - 1, CT - 1)
                    wait_count(act, v_stored, 16 * b)
                    for j in range(TT):
                        i = CT + j
                        act.wait_ge(out_ready, OUTS * t + i + 1)
                        act.activation(v_out[:, :, u * TT + j, :], out_ps[:, i % 4, :].rearrange("p (h d) -> p h d", h=H),
                                       ACT.Copy).then_inc(act_out, 1)
                    if u == HB - 1:
                        act.wait_ge(act_out, OUTS * t + 2 * CT)
                        act.dma_start(v_scr[b, :, :, :].rearrange("h p n -> p h n"),
                                      v_out[:, :, :, :].rearrange("p h j d -> p h (j d)")).then_inc(v_stored, 16)
                    for ct in range(CT):
                        take_hi(t, 2 * CT + ct, CT + ct)
                        if ct:
                            store(q_scr, t, b, u, ct - 1, CT + ct - 1)
                    store(q_scr, t, b, u, CT - 1, 2 * CT - 1)

            repeat(act, B, body)
            for i in range(4):
                act.wait_ge(qk_stored[i], 16 * 2 * B * HB)
            act.wait_ge(v_stored, 16 * B)

        @block.vector
        def _(dve):
            def split_weight(hi, lo, w):
                n = split_weight.n = split_weight.n + 1
                dve.tensor_copy(hi, w).then_inc(w_hi_ready, 1)
                dve.wait_ge(w_hi_ready, n)
                dve.tensor_tensor(lo, w, raw(hi), ALU.subtract).then_inc(w_lo_ready, 1)
            split_weight.n = 0

            def prepare_ctx(t, u, b):
                dve.wait_ge(c_loaded[u], 16 * (b + 1))
                wait_count(dve, out_ready, OUTS * t - CT)
                dve.tensor_copy(c_hi[:, :, :], cin[:, u, :, :]).then_inc(c_hi_ready, 1)

            def prepare_x(t, u, b):
                dve.wait_ge(x_loaded[u], 16 * (b + 1))
                for j in range(TT):
                    last = dve.bn_stats(stats[:, j, :], xin[:, u, j, :])
                last.then_inc(stats_ready, 1)
                wait_apart(dve, stats_ready, t + 1)
                for j in range(TT):
                    last = dve.bn_aggr(moments[:, j, :], stats[:, j, :])
                last.then_inc(moments_ready, 1)
                dve.wait_ge(moments_ready, t + 1)
                wait_count(dve, rstd_ready, t)
                dve.tensor_scalar(var_eps[:, :], moments[:, :, 1], EPS, None, ALU.add).then_inc(eps_added, 1)
                dve.wait_ge(rstd_ready, t + 1)
                wait_count(dve, zT_ready, CT * t)
                for j in range(TT):
                    last = dve.tensor_scalar(z[:, j, :], xin[:, u, j, :], moments[:, j, 0:1], rstd[:, j:j + 1],
                                             ALU.subtract, ALU.mult)
                last.then_inc(z_ready, 1)

            def take_lo(t, i, s):
                dve.wait_ge(act_out, OUTS * t + i + 1)
                dve.tensor_tensor(qk_out[:, s % 4, 1, :], out_ps[:, i % 4, :], raw(qk_out[:, s % 4, 0, :]),
                                  ALU.subtract).then_inc(dve_out, 1)

            dve.wait_ge(wk_loaded, 16)
            split_weight(wkv_hi[:, :, 0:D], wkv_lo[:, :, 0:D], wkv_raw[:, :, 0:D])
            prepare_ctx(0, 0, 0)
            dve.wait_ge(c_hi_ready, 1)
            dve.tensor_tensor(c_lo[:, 0:CT // 2, :], cin[:, 0, 0:CT // 2, :], raw(c_hi[:, 0:CT // 2, :]), ALU.subtract
                              ).then_inc(c_lo_first, 1)
            dve.wait_ge(wv_loaded, 16)
            split_weight(wkv_hi[:, :, D:2 * D], wkv_lo[:, :, D:2 * D], wkv_raw[:, :, D:2 * D])
            prepare_x(0, 0, 0)
            dve.wait_ge(wq_loaded, 16)
            split_weight(wq_hi[:, :, :], wq_lo[:, :, :], wq_raw[:, :, :])

            def body(b):
                for u in range(HB):
                    t = HB * b + u
                    for i in range(CT):
                        take_lo(t, i, i)
                    for ct in range(CT):
                        dve.wait_ge(z_hi_ready, CT * t + ct + 1)
                        dve.tensor_tensor(z_lo[:, ct, :], zT_ps[:, ct % 2, :], raw(z_hi[:, ct, :]),
                                          ALU.subtract).then_inc(z_lo_ready, 1)
                    if not (is_last(b, B) and u == HB - 1):
                        nu, nb = (u + 1) % HB, b + (u + 1) // HB
                        prepare_ctx(t + 1, nu, nb)
                        prepare_x(t + 1, nu, nb)
                    for ct in range(CT):
                        take_lo(t, 2 * CT + ct, CT + ct)

            repeat(dve, B, body)

        @block.tensor
        def _(pe):
            def product(t, i, lhs, rhs):
                o = OUTS * t + i
                wait_count(pe, act_out, o - 3)
                for ct in range(CT):
                    for n, (a, m) in enumerate(((0, 0), (0, 1), (1, 0))):
                        last = pe.matmul(out_ps[:, i % 4, :], lhs(a, ct), rhs(m, ct),
                                         start=(ct == 0 and n == 0), stop=(ct == CT - 1 and n == 2))
                last.then_inc(out_ready, 1)

            w_kv, w_q, cs, zs = (wkv_hi, wkv_lo), (wq_hi, wq_lo), (c_hi, c_lo), (z_hi, z_lo)

            def body(b):
                for u in range(HB):
                    t = HB * b + u
                    first = isinstance(b, int) and t == 0
                    if first:
                        pe.wait_ge(w_lo_ready, 1)
                        pe.wait_ge(c_lo_first, 1)
                    pe.wait_ge(c_lo_ready, t + 1)
                    for i in range(CT):
                        wait_count(pe, dve_out, 2 * CT * t - (CT - 1) + i)
                        product(t, i, lambda a, ct: w_kv[a][:, ct, i * P:(i + 1) * P], lambda m, ct: cs[m][:, ct, :])
                    if first:
                        pe.wait_ge(ident_ready, 2)
                    pe.wait_ge(z_ready, t + 1)
                    for j in range(TT):
                        for ct in ((0, 1), (2, 3), (), ())[j]:
                            wait_count(pe, z_lo_ready, CT * t + ct - 1)
                            for r in range(TT):
                                last = pe.transpose(zT_ps[:, ct % 2, r * P:(r + 1) * P], z[:, r, ct * P:(ct + 1) * P],
                                                    ident[:, :])
                            last.then_inc(zT_ready, 1)
                        if first and j == 0:
                            pe.wait_ge(w_lo_ready, 2)
                        pe.wait_ge(dve_out, 2 * CT * t + j + 1)
                        product(t, CT + j, lambda a, ct: cs[a][:, ct, j * P:(j + 1) * P],
                                lambda m, ct: w_kv[m][:, ct, D:2 * D])
                    if first:
                        pe.wait_ge(w_lo_ready, 3)
                    pe.wait_ge(z_lo_ready, CT * (t + 1))
                    for ot in range(CT):
                        product(t, 2 * CT + ot, lambda a, ct: w_q[a][:, ct, ot * P:(ot + 1) * P],
                                lambda m, ct: zs[m][:, ct, :])

            repeat(pe, B, body)


def attention(nc, bias, Wproj, q_scr, k_scr, v_scr, y_scr, ident, proj, B, T, S, H, DH, INV_SCALE):
    NQ, NKT = T // P, S // P
    TILES = B * NQ
    LAG = 4
    PV0 = NQ + LAG + 2
    KEYS_AT = ((0,), (1, 2), (3,), (4,), (5,), (6,), (7,), ())
    NX = 8
    QW = T // 4
    with ExitStack() as c:
        def sb(name, shape, dt=F32):
            return c.enter_context(nc.sbuf_tensor(name, shape, dt))

        def sem(name):
            return c.enter_context(nc.semaphore(name))

        bias_sb = sb("bias_sb", [P, NQ, S])
        q_pack = sb("q_pack", [P, B, T], F32R)
        k_pack = sb("k_pack", [P, B, S], F32R)
        v_sb = sb("v_sb", [P, B, NKT, DH])
        xs = sb("xs", [P, NX, S])
        row_max, exp_bias = sb("row_max", [P, NX]), sb("exp_bias", [P, NX])
        row_sum, inv_sum = sb("row_sum", [P, NX]), sb("inv_sum", [P, NX])
        probsT = sb("probsT", [P, 2, NKT, T])
        y_stage = proj.y_stage
        scores_ps = c.enter_context(nc.psum_tensor("scores_ps", [P, 2, S], F32))
        pT_ps = c.enter_context(nc.psum_tensor("pT_ps", [P, 3, TB], F32))
        y_ps = c.enter_context(nc.psum_tensor("y_ps2", [P, TB], F32))

        pack_loaded = [sem(f"pack_loaded{b}") for b in range(B)]
        v_loaded = [sem(f"v_loaded{b}") for b in range(B)]
        bias_loaded = [sem(f"bias_loaded{i}") for i in range(NQ)]
        scores_ready, biased, exp_bias_ready = sem("scores_ready"), sem("biased"), sem("exp_bias_ready")
        exp_ready, inverted, normalised, pT_ready = sem("exp_ready"), sem("inverted"), sem("normalised"), sem("pT_ready")
        dve_copied, act_copied = sem("dve_copied"), sem("act_copied")
        pv_ready, y_taken = sem("pv_ready"), sem("y_taken")
        y_stored = proj.y_stored
        block = c.enter_context(nc.Block())

        def pT_bank(j, half):
            return j % 2 if half else 2

        def copy_half(eng, copy, done, h, j, half):
            if isinstance(h, int) and TILES * h + j < LAG:
                return
            n, jt = TILES * h + j - LAG, (j - LAG) % TILES
            b, qt = jt // NQ, jt % NQ
            if qt == 0:
                wait_count(eng, pv_ready, (B * h + b - 1) if j >= LAG else (B * (h - 1) + b - 1))
            eng.wait_ge(pT_ready, 2 * n + half + 1)
            copy(probsT[:, b % 2, half * 4:half * 4 + 4, qt * P:(qt + 1) * P],
                 pT_ps[:, pT_bank(jt, half), :].rearrange("p (k q) -> p k q", q=P)).then_inc(done, 1)

        @block.sync
        def _(sp):
            def load_pack(h, b):
                wait_count(sp, scores_ready, TILES * (h - 1) + NQ * (b + 1))
                for l in range(2):
                    rows = slice(64 * l, 64 * l + 64)
                    sp.dma_start(raw(q_pack[rows, b, :]),
                                 q_scr[b, bass.ds(h * DH, DH), :, :].rearrange("d m t -> (d m) t")
                                 ).then_inc(pack_loaded[b], 16)
                    k_rows = k_scr[b, bass.ds(h * DH, DH), l:l + 1, :]
                    sp.dma_start(raw(k_pack[rows, b, :]), k_rows.broadcast_to([DH, 2, S])).then_inc(pack_loaded[b], 16)

            def load_v(h, b):
                wait_count(sp, pv_ready, B * (h - 1) + b + 1)
                sp.dma_start(v_sb[:, b, :, :].rearrange("p k d -> p (k d)"),
                             v_scr[b, bass.ds(h, 1), :, :].rearrange("h p n -> (h p) n")).then_inc(v_loaded[b], 16)

            def load_bias(h, qt):
                wait_count(sp, biased, TILES * (h - 1) + (B - 1) * NQ + qt + 1)
                sp.dma_start(bias_sb[:, qt, :],
                             bias[0, bass.ds(h, 1), qt * P:(qt + 1) * P, :].rearrange("h p s -> (h p) s")
                             ).then_inc(bias_loaded[qt], 16)

            def body(h):
                load_pack(h, 0)
                if isinstance(h, int) and h == 0:
                    load_bias(h, 0)
                    load_bias(h, 1)
                    load_bias(h, 2)
                    load_v(h, 0)
                    for qt in range(3, NQ):
                        load_bias(h, qt)
                    load_pack(h, 1)
                    load_v(h, 1)
                    for b in (2, 3):
                        load_pack(h, b)
                        load_v(h, b)
                    return
                load_pack(h, 1)
                load_v(h, 0)
                load_pack(h, 2)
                load_bias(h, 0)
                load_bias(h, 1)
                load_v(h, 1)
                for qt in range(2, NQ):
                    load_bias(h, qt)
                load_pack(h, 3)
                load_v(h, 2)
                load_v(h, 3)

            repeat(sp, H, body)
            sp.dma_start(proj.wp_raw[:, :, :], Wproj.rearrange("(c p) n -> p c n", p=P)).then_inc(proj.wp_loaded, 16)
            sp.wait_ge(y_stored[0], 64 * (B * (H - 1) // 2 + 1))
            for u in range(proj.y.shape[1]):
                load_y(sp, proj, y_scr, 0, u)

        @block.gpsimd
        def _(pool):
            def normalise(n, i):
                wait_apart(pool, inverted, n + 1)
                pool.tensor_scalar(xs[:, i, :], xs[:, i, :], inv_sum[:, i:i + 1], 0.0, ALU.mult, ALU.add
                                   ).then_inc(normalised, 1)

            def body(h):
                for j in range(TILES):
                    n, i = TILES * h + j, j % NX
                    wait_apart(pool, biased, n + 1)
                    pool.tensor_scalar(exp_bias[:, i:i + 1], row_max[:, i:i + 1], -INV_SCALE, 0.0, ALU.mult, ALU.add
                                       ).then_inc(exp_bias_ready, 1)
                    if not (isinstance(h, int) and n < 2):
                        normalise(n - 2, (j - 2) % NX)

            repeat(pool, H, body)
            for i in (NX - 2, NX - 1):
                normalise(TILES * H - NX + i, i)

        @block.vector
        def _(dve):
            def invert(n, i):
                dve.wait_ge(exp_ready, n + 1)
                dve.reciprocal(inv_sum[:, i:i + 1], row_sum[:, i:i + 1]).then_inc(inverted, 1)

            def body(h):
                for j in range(TILES):
                    n = TILES * h + j
                    b, qt = j // NQ, j % NQ
                    if b == 0:
                        dve.wait_ge(bias_loaded[qt], 16 * (h + 1))
                    wait_count(dve, pT_ready, 2 * (n - NX + 1))
                    wait_apart(dve, scores_ready, n + 1)
                    dve.tensor_tensor_reduce(out=xs[:, j % NX, :], in0=scores_ps[:, j % 2, :], in1=bias_sb[:, qt, :],
                                             scale=1.0, scalar=-3.4e38, op0=ALU.add, op1=ALU.max,
                                             accum_out=row_max[:, j % NX:j % NX + 1]).then_inc(biased, 1)
                    copy_half(dve, dve.tensor_copy, dve_copied, h, j, 0)
                    if not (isinstance(h, int) and n < 2):
                        invert(n - 2, (j - 2) % NX)

            repeat(dve, H, body)
            for i in (NX - 2, NX - 1):
                invert(TILES * H - NX + i, i)
            for j in range(LAG):
                copy_half(dve, dve.tensor_copy, dve_copied, H, j, 0)
            dve.wait_ge(proj.wp_loaded, 16)
            dve.tensor_copy(proj.wp_hi[:, :, :], proj.wp_raw[:, :, :]).then_inc(proj.wp_hi_ready, 1)
            dve.wait_ge(proj.wp_hi_ready, 1)
            dve.tensor_tensor(proj.wp_lo[:, :, :], proj.wp_raw[:, :, :], raw(proj.wp_hi[:, :, :]), ALU.subtract
                              ).then_inc(proj.wp_ready, 1)

        @block.scalar
        def _(act):
            def copy(out, in_):
                return act.activation(out, in_, ACT.Copy)

            def take_output(group, slot):
                act.wait_ge(pv_ready, group + 1)
                wait_count(act, y_stored[slot], 32 * (group - slot))
                act.activation(y_stage[:, slot, :], y_ps[:, 0:QW], ACT.Copy).then_inc(y_taken, 1)

            def store_output(group, slot, b, h):
                act.wait_ge(y_taken, group + 1)
                for q in range(4):
                    act.dma_start(y_scr[b, q, bass.ds(h * DH, DH), :], y_stage[DH * q:DH * q + DH, slot, :]
                                  ).then_inc(y_stored[slot], 16)

            def body(h):
                for j in range(TILES):
                    n, i = TILES * h + j, j % NX
                    b, qt = j // NQ, j % NQ
                    act.wait_ge(exp_bias_ready, n + 1)
                    act.activation(xs[:, i, :], xs[:, i, :], ACT.Exp, bias=exp_bias[:, i:i + 1], scale=INV_SCALE,
                                   accum_out=row_sum[:, i:i + 1]).then_inc(exp_ready, 1)
                    copy_half(act, copy, act_copied, h, j, 1)
                    if not (isinstance(h, int) and h == 0 and b < 2):
                        if qt == 3:
                            take_output(B * h + b - 2, b % 2)
                        elif qt == 5:
                            store_output(B * h + b - 2, b % 2, (b - 2) % B, h if b >= 2 else h - 1)

            repeat(act, H, body)
            for j in range(LAG):
                copy_half(act, copy, act_copied, H, j, 1)
            for b in (B - 2, B - 1):
                take_output(B * (H - 1) + b, b % 2)
                store_output(B * (H - 1) + b, b % 2, b, H - 1)

        @block.tensor
        def _(pe):
            def scores(n, j, h):
                b, qt = j // NQ, j % NQ
                if qt == 0:
                    pe.wait_ge(pack_loaded[b], 64 * (h + 1))
                wait_count(pe, biased, n - 1)
                for half in range(2):
                    last = pe.matmul(scores_ps[:, j % 2, half * TB:(half + 1) * TB],
                                     q_pack[:, b, qt * P:(qt + 1) * P], k_pack[:, b, half * TB:(half + 1) * TB],
                                     start=True, stop=True)
                last.then_inc(scores_ready, 1)

            def transposes(n, j):
                pe.wait_ge(normalised, n + 1)
                for half, copied in enumerate((dve_copied, act_copied)):
                    wait_count(pe, copied, n - 1 if half == 1 else n)
                    for k in range(4):
                        kt = 4 * half + k
                        last = pe.transpose(pT_ps[:, pT_bank(j, half), k * P:(k + 1) * P],
                                            xs[:, j % NX, kt * P:(kt + 1) * P], ident[:, :])
                    last.then_inc(pT_ready, 1)

            def outputs(group, b, kt, h):
                if kt == 0:
                    pe.wait_ge(dve_copied, NQ * (group + 1))
                    pe.wait_ge(act_copied, NQ * (group + 1))
                    pe.wait_ge(v_loaded[b], 16 * (h + 1))
                    wait_count(pe, y_taken, group)
                for q in range(4):
                    last = pe.matmul(y_ps[DH * q:DH * q + DH, 0:QW], v_sb[:, b, kt, :],
                                     probsT[:, b % 2, kt, q * QW:(q + 1) * QW],
                                     start=(kt == 0), stop=(kt == NKT - 1))
                if kt == NKT - 1:
                    last.then_inc(pv_ready, 1)

            def outputs_at(h, j):
                back = j - PV0
                h_of = h if back >= 0 else h - 1
                b, at = (back % TILES) // NQ, back % NQ
                for kt in KEYS_AT[at]:
                    outputs(B * h_of + b, b, kt, h_of)

            def body(h):
                for j in range(TILES):
                    n = TILES * h + j
                    scores(n, j, h)
                    if not (isinstance(h, int) and n < PV0):
                        outputs_at(h, j)
                    if not (isinstance(h, int) and n < LAG):
                        transposes(n - LAG, (j - LAG) % TILES)

            repeat(pe, H, body)
            for j in range(PV0):
                if j < LAG:
                    transposes(TILES * H + j - LAG, TILES + j - LAG)
                outputs_at(H, j)


def load_y(sp, proj, y_scr, b, u):
    for q in range(2):
        sp.dma_start(proj.y[:, u, :, q * (TB // 2):(q + 1) * (TB // 2)],
                     y_scr[b, 2 * u + q, :, :].rearrange("(c p) t -> p c t", p=P)).then_inc(proj.y_loaded[u], 16)


def project_out(nc, x, g_xattn, Wr, br, y_scr, x1_scr, z2_scr, ident, experts, proj, ffn):
    B, T, D = x.shape
    CT, HB, NE, H = D // P, T // TB, Wr.shape[1], D // 32
    NT = B * HB
    with ExitStack() as c:
        def sb(name, shape, dt=F32):
            return c.enter_context(nc.sbuf_tensor(name, shape, dt))

        def sem(name):
            return c.enter_context(nc.semaphore(name))

        wp_hi, wp_lo, y = proj.wp_hi, proj.wp_lo, proj.y
        wr_sb = sb("wr_sb", [P, CT, NE])
        br_sb = sb("br_sb", [1, NE])
        gate, gate_t = sb("gate", [P, 1]), sb("gate_t", [P, 1])
        x_in = sb("x_in3", [P, HB, TT, D])
        y_hi, y_lo = sb("y_hi", [P, HB, CT, TB], F32R), sb("y_lo", [P, HB, CT, TB], F32R)
        x1, zT = ffn.x1, ffn.z2T
        z2 = sb("z2", [P, TT, D])
        stats = sb("stats3", [P, TT, 6])
        moments = sb("moments3", [P, TT, 2])
        var_eps = sb("var_eps3", [P, TT])
        rstd, shift = sb("rstd3", [P, TT]), sb("shift3", [P, TT])
        minus_half = sb("minus_half3", [P, TT])
        z_sum = sb("z_sum", [P, CT, B, HB])
        z_tot = sb("z_tot", [P, CT, B])
        route = sb("route", [1, B, NE])
        best = sb("best", [1, B, 8])
        y_ps = c.enter_context(nc.psum_tensor("y_ps", [P, 4, D], F32))
        zT_ps = c.enter_context(nc.psum_tensor("zT_ps3", [P, 2, TB], F32))
        route_ps = c.enter_context(nc.psum_tensor("route_ps", [1, B, NE], F32))

        small_loaded = sem("small_loaded")
        y_loaded = proj.y_loaded
        x_loaded = [sem(f"x_loaded3{u}") for u in range(HB)]
        gate_ready, const_ready = sem("gate_ready"), sem("const3")
        y_hi_ready, y_lo_ready, y_done = sem("y_hi_ready"), sem("y_lo_ready"), sem("y_done")
        y_lo_first = sem("y_lo_first")
        x1_ready, stats_ready, moments_ready, eps_added = sem("x1_ready"), sem("stats_ready3"), sem("moments3s"), sem("eps3")
        rstd_ready, z_ready, zT_ready = sem("rstd3s"), sem("z_ready3"), sem("zT_ready3")
        shift_ready, zT_taken = sem("shift_ready"), sem("zT_taken")
        x1_stored, z_stored = ffn.x1_stored, ffn.z_stored
        tot_ready, route_done, route_ready, best_ready, expert_ready = (
            sem("tot_ready"), sem("route_done"), sem("route_ready"), sem("best_ready"), sem("expert_ready"))
        block = c.enter_context(nc.Block())

        @block.sync
        def _(sp):
            sp.dma_start(gate[:, :], g_xattn.rearrange("(a e) -> a e", a=1).broadcast_to([P, 1])).then_inc(small_loaded, 16)
            sp.dma_start(wr_sb[:, :, :], Wr.rearrange("(c p) e -> p c e", p=P)).then_inc(small_loaded, 16)
            sp.dma_start(br_sb[:, :], br.rearrange("(a e) -> a e", a=1)).then_inc(small_loaded, 16)

            def loads(b):
                for u in range(HB):
                    t = HB * b + u
                    if not (isinstance(b, int) and b == 0):
                        for i in range(2):
                            sp.wait_ge(proj.y_stored[i], 64 * B * H // 2)
                        sp.wait_ge(y_lo_first, 1)
                        sp.wait_ge(y_lo_ready, t - 1 - u)
                        load_y(sp, proj, y_scr, b, u)
                    wait_count(sp, x1_ready, TT * (t - 1))
                    sp.dma_start(x_in[:, u, :, :], x[b, u * TB:(u + 1) * TB, :].rearrange("(j p) n -> p j n", p=P)
                                 ).then_inc(x_loaded[u], 16)

                if is_last(b, B):
                    sp.wait_ge(z_stored[0], 16)
                    ffn.load(sp, z2_scr, 0)

            repeat(sp, B, loads)

        @block.gpsimd
        def _(pool):
            pool.memset(minus_half[:, :], -0.5).then_inc(const_ready, 1)
            pool.wait_ge(const_ready, 1)

            def y_lo_of(t, u):
                pool.wait_ge(y_hi_ready, t + 1)
                pool.tensor_tensor(y_lo[:, u, :, :], y[:, u, :, :], raw(y_hi[:, u, :, :]), ALU.subtract
                                   ).then_inc(y_lo_ready, 1)

            y_lo_of(1, 1)

            def body(b):
                for u in range(HB):
                    t = HB * b + u
                    pool.wait_ge(eps_added, t + 1)
                    pool.tensor_tensor(rstd[:, :], var_eps[:, :], minus_half[:, :], ALU.pow).then_inc(rstd_ready, 1)
                    pool.wait_ge(rstd_ready, t + 1)
                    pool.tensor_tensor(shift[:, :], moments[:, :, 0], rstd[:, :], ALU.mult).then_inc(shift_ready, 1)
                    wait_apart(pool, shift_ready, 2 * t + 1)
                    pool.tensor_scalar(shift[:, :], shift[:, :], -1.0, 0.0, ALU.mult, ALU.add).then_inc(shift_ready, 1)
                    wait_count(pool, zT_ready, CT * t)
                    wait_apart(pool, shift_ready, 2 * t + 2)
                    for j in range(TT):
                        last = pool.tensor_scalar(z2[:, j, :], x1[:, u, j, :], rstd[:, j:j + 1], shift[:, j:j + 1],
                                                  ALU.mult, ALU.add)
                    last.then_inc(z_ready, 1)
                    if not is_last(b, B):
                        y_lo_of(t + 2, u)

            repeat(pool, B, body)

        @block.scalar
        def _(act):
            def y_hi_of(t, b, u):
                act.wait_ge(y_loaded[u], 32 * (b + 1))
                wait_count(act, y_done, TT * (t - 1))
                act.activation(y_hi[:, u, :, :], y[:, u, :, :], ACT.Copy).then_inc(y_hi_ready, 1)

            y_hi_of(0, 0, 0)
            y_hi_of(1, 0, 1)
            act.wait_ge(small_loaded, 48)
            act.activation(gate_t[:, :], gate[:, :], ACT.Tanh).then_inc(gate_ready, 1)

            def body(b):
                for u in range(HB):
                    t = HB * b + u
                    if is_last(b, B) and u == 0:
                        ffn.split_hi(act, 0, 0)
                    act.wait_ge(x1_ready, TT * (t + 1))
                    act.dma_start(x1_scr[bass.ds(t * TB, TB), :].rearrange("(j p) n -> p j n", p=P), x1[:, u, :, :]
                                  ).then_inc(x1_stored[u], 16)
                    if not is_last(b, B):
                        y_hi_of(t + 2, b + 1, u)
                    wait_count(act, z_stored[u], 16 * b)
                    for ct in range(CT):
                        act.wait_ge(zT_ready, CT * t + ct + 1)
                        act.activation(zT[:, u, ct, :], zT_ps[:, ct % 2, :], ACT.Copy,
                                       accum_out=z_sum[:, ct, b, u:u + 1] if isinstance(b, int)
                                       else z_sum[:, ct, bass.ds(b, 1), u]).then_inc(zT_taken, 1)
                    act.wait_ge(zT_taken, CT * (t + 1))
                    act.dma_start(z2_scr[bass.ds(t, 1), :, :, :].rearrange("a p c t -> (a p) c t"), zT[:, u, :, :]
                                  ).then_inc(z_stored[u], 16)

            repeat(act, B, body)

        @block.vector
        def _(dve):
            dve.wait_ge(y_hi_ready, 1)
            dve.tensor_tensor(y_lo[:, 0, :, :], y[:, 0, :, :], raw(y_hi[:, 0, :, :]), ALU.subtract).then_inc(y_lo_first, 1)
            dve.wait_ge(gate_ready, 1)

            def body(b):
                for u in range(HB):
                    t = HB * b + u
                    dve.wait_ge(x_loaded[u], 16 * (b + 1))
                    wait_count(dve, x1_stored[u], 16 * b)
                    wait_count(dve, z_ready, t - 1)
                    for j in range(TT):
                        dve.wait_ge(y_done, TT * t + j + 1)
                        dve.scalar_tensor_tensor(x1[:, u, j, :], y_ps[:, j, :], gate_t[:, 0:1], x_in[:, u, j, :],
                                                 ALU.mult, ALU.add).then_inc(x1_ready, 1)
                        if j:
                            dve.wait_ge(x1_ready, TT * t + j)
                            dve.bn_stats(stats[:, j - 1, :], x1[:, u, j - 1, :]).then_inc(stats_ready, 1)
                    dve.wait_ge(x1_ready, TT * (t + 1))
                    dve.bn_stats(stats[:, TT - 1, :], x1[:, u, TT - 1, :]).then_inc(stats_ready, 1)
                    wait_apart(dve, stats_ready, TT * (t + 1))
                    if not (isinstance(t, int) and t == 0):
                        wait_apart(dve, shift_ready, 2 * t - 1)
                    for j in range(TT):
                        last = dve.bn_aggr(moments[:, j, :], stats[:, j, :])
                    last.then_inc(moments_ready, 1)
                    dve.wait_ge(moments_ready, t + 1)
                    wait_count(dve, rstd_ready, t)
                    dve.tensor_scalar(var_eps[:, :], moments[:, :, 1], EPS, None, ALU.add).then_inc(eps_added, 1)
                    if is_last(b, B) and u == 0:
                        ffn.split_lo(dve, 0, 0)

            repeat(dve, B, body)
            dve.wait_ge(zT_taken, CT * NT)
            dve.tensor_tensor(z_tot[:, :, :], z_sum[:, :, :, 0], z_sum[:, :, :, 1], ALU.add).then_inc(tot_ready, 1)
            dve.wait_ge(route_done, 1)
            dve.wait_ge(small_loaded, 48)
            for b in range(B):
                last = dve.scalar_tensor_tensor(route[:, b, :], route_ps[:, b, :], 1.0 / T, br_sb[:, :],
                                                ALU.mult, ALU.add)
            last.then_inc(route_ready, 1)
            dve.wait_ge(route_ready, 1)
            for b in range(B):
                last = dve.max(best[:, b, :], route[:, b, :])
            last.then_inc(best_ready, 1)
            dve.wait_ge(best_ready, 1)
            for b in range(B):
                last = dve.max_index(experts[:, b, :], best[:, b, :], route[:, b, :])
            last.then_inc(expert_ready, 1)

        @block.tensor
        def _(pe):
            def product(t, u, j):
                wait_count(pe, x1_ready, TT * (t - 1) + j + 1)
                for ct in range(CT):
                    for n, (a, w) in enumerate(((y_hi, wp_hi), (y_hi, wp_lo), (y_lo, wp_hi))):
                        last = pe.matmul(y_ps[:, j, :], a[:, u, ct, j * P:(j + 1) * P], w[:, ct, :],
                                         start=(ct == 0 and n == 0), stop=(ct == CT - 1 and n == 2))
                last.then_inc(y_done, 1)

            def transposes(t, ct):
                wait_count(pe, zT_taken, CT * t + ct - 1)
                for j in range(TT):
                    last = pe.transpose(zT_ps[:, ct % 2, j * P:(j + 1) * P], z2[:, j, ct * P:(ct + 1) * P], ident[:, :])
                last.then_inc(zT_ready, 1)

            pe.wait_ge(proj.wp_ready, 1)
            pe.wait_ge(y_lo_first, 1)
            for j in range(TT):
                product(0, 0, j)

            def body(b):
                for u in range(HB):
                    t = HB * b + u
                    more = not (is_last(b, B) and u == HB - 1)
                    if more:
                        pe.wait_ge(y_lo_ready, t + 1)
                        for j in range(TT - 1):
                            product(t + 1, (u + 1) % HB, j)
                    pe.wait_ge(z_ready, t + 1)
                    transposes(t, 0)
                    transposes(t, 1)
                    if more:
                        product(t + 1, (u + 1) % HB, TT - 1)
                    transposes(t, 2)
                    transposes(t, 3)

            repeat(pe, B, body)
            pe.wait_ge(tot_ready, 1)
            pe.wait_ge(small_loaded, 48)
            for b in range(B):
                for ct in range(CT):
                    last = pe.matmul(route_ps[:, b, :], z_tot[:, ct, b:b + 1], wr_sb[:, ct, :],
                                     start=(ct == 0), stop=(ct == CT - 1))
            last.then_inc(route_done, 1)


def expert_ffn(nc, g_ffn, W1c, b1c, W2, b2, x1_scr, z2_scr, experts, out, ffn, B, T):
    NE, NF, _, D = W1c.shape
    CT, HB = D // P, T // TB
    NW = 4
    with ExitStack() as c:
        def sb(name, shape, dt=F32):
            return c.enter_context(nc.sbuf_tensor(name, shape, dt))

        def sem(name):
            return c.enter_context(nc.semaphore(name))

        w_raw = sb("w_raw", [P, NW, 2, D])
        w_hi, w_lo = sb("w_hi", [P, NW, 2, D], F32R), sb("w_lo", [P, NW, 2, D], F32R)
        zT = ffn.zT
        h_full = sb("h_full", [P, 2, TB])
        h_hi, h_lo = sb("h_hi", [P, 2, TB], F32R), sb("h_lo", [P, 2, TB], F32R)
        x1 = ffn.x1
        b1_sb = sb("b1_sb", [P, B, NF])
        b2_sb = sb("b2_sb", [P, B, D])
        b2_gated = sb("b2_gated", [P, D])
        gate, gate_t = sb("gate4", [P, 1]), sb("gate_t4", [P, 1])
        h_ps = c.enter_context(nc.psum_tensor("h_ps", [P, 2, TB], F32))
        y_ps = c.enter_context(nc.psum_tensor("y_ps4", [P, TT, D], F32))

        w_loaded = [sem(f"w_loaded{i}") for i in range(NW)]
        z_lo_ready = ffn.z_lo_ready
        x1_loaded = [sem(f"x1_loaded{u}") for u in range(HB)]
        b_loaded = sem("b_loaded")
        gate_loaded, gate_ready = sem("gate_loaded"), sem("gate_ready4")
        b2_ready, x1_biased = sem("b2_ready"), sem("x1_biased")
        w_hi_ready, w_lo_ready = sem("w_hi4"), sem("w_lo4")
        hT_ready, h_hi_ready, h_lo_ready = sem("hT_ready"), sem("h_hi4"), sem("h_lo4")
        chunk_done, y_done, res_ready = sem("chunk_done"), sem("y_done4"), sem("res_ready")
        out_stored = [sem(f"out_stored{u}") for u in range(HB)]
        block = c.enter_context(nc.Block())

        @block.sync
        def _(sp):
            sp.dma_start(gate[:, :], g_ffn.rearrange("(a e) -> a e", a=1).broadcast_to([P, 1])).then_inc(gate_loaded, 16)

            def body(b):
                e = sp.value_load(experts[0:1, bass.ds(b, 1), 0:1].rearrange("p a e -> p (a e)"), min_val=0, max_val=NE - 1)
                for u in range(HB):
                    t = HB * b + u
                    for f in range(NF):
                        slot = f % NW
                        wait_count(sp, w_lo_ready, NF * t + f - NW + 1)
                        sp.dma_start(w_raw[:, slot, 0, :], W1c[bass.ds(e, 1), f, :, :].rearrange("a p n -> (a p) n")
                                     ).then_inc(w_loaded[slot], 16)
                        sp.dma_start(w_raw[:, slot, 1, :], W2[bass.ds(e, 1), f * P:(f + 1) * P, :
                                                             ].rearrange("a p n -> (a p) n")
                                     ).then_inc(w_loaded[slot], 16)
                        if u == 0 and f == 0:
                            sp.dma_start(b1_sb[:, bass.ds(b, 1), :], b1c[bass.ds(e, 1), :, :].rearrange("a p f -> p a f")
                                         ).then_inc(b_loaded, 16)
                            sp.dma_start(b2_sb[:, bass.ds(b, 1), :], b2[bass.ds(e, 1), :].rearrange("(c a) n -> c a n", c=1
                                                                                                   ).broadcast_to([P, 1, D])
                                         ).then_inc(b_loaded, 16)
                        if f == NW and not (is_last(b, B) and u == HB - 1):
                            sp.wait_ge(z_lo_ready, t + 1)
                            sp.wait_ge(ffn.z_stored[1 - u], 16 * (b + 1 + u))
                            ffn.load(sp, z2_scr, t + 1)
                        if f == NW:
                            if u == 0:
                                sp.wait_ge(b_loaded, 32 * (b + 1))
                            wait_count(sp, out_stored[u], 16 * b)
                            sp.wait_ge(ffn.x1_stored[u], 16 * B)
                            sp.dma_start(x1[:, u, :, :], x1_scr[bass.ds(t * TB, TB), :
                                                               ].rearrange("(j p) n -> p j n", p=P)
                                         ).then_inc(x1_loaded[u], 16)

            repeat(sp, B, body)

        @block.gpsimd
        def _(pool):
            pool.wait_ge(gate_ready, 1)

            def body(b):
                pool.wait_ge(b_loaded, 32 * (b + 1))
                wait_count(pool, x1_biased, HB * b)
                pool.tensor_tensor(b2_gated[:, :], b2_sb[:, bass.ds(b, 1), :].rearrange("p a n -> p (a n)"),
                                   gate_t[:, 0:1].broadcast_to([P, D]), ALU.mult).then_inc(b2_ready, 1)
                pool.wait_ge(b2_ready, b + 1)
                for u in range(HB):
                    t = HB * b + u
                    pool.wait_ge(x1_loaded[u], 16 * (b + 1))
                    for j in range(TT):
                        last = pool.tensor_tensor(x1[:, u, j, :], x1[:, u, j, :], b2_gated[:, :], ALU.add)
                    last.then_inc(x1_biased, 1)

            repeat(pool, B, body)

        @block.scalar
        def _(act):
            act.wait_ge(gate_loaded, 16)
            act.activation(gate_t[:, :], gate[:, :], ACT.Tanh).then_inc(gate_ready, 1)

            def store(t, u):
                act.wait_ge(res_ready, TT * (t + 1))
                act.dma_start(out[bass.ds(t * TB, TB), :].rearrange("(j p) n -> p j n", p=P), x1[:, u, :, :]
                              ).then_inc(out_stored[u], 16)

            def body(b):
                act.wait_ge(b_loaded, 32 * (b + 1))
                for u in range(HB):
                    t = HB * b + u
                    for f in range(NF):
                        n = NF * t + f
                        b1 = b1_sb[:, bass.ds(b, 1), f:f + 1].rearrange("p a f -> p (a f)")
                        wait_count(act, h_lo_ready, n - 1)
                        wait_apart(act, hT_ready, n + 1)
                        act.activation(h_full[:, f % 2, :], h_ps[:, f % 2, :], ACT.Relu, bias=b1)
                        if not (isinstance(n, int) and n < 2):
                            wait_apart(act, chunk_done, n - 1)
                        act.activation(h_hi[:, f % 2, :], h_ps[:, f % 2, :], ACT.Relu, bias=b1).then_inc(h_hi_ready, 1)
                        if f == 2 and not (isinstance(t, int) and t == 0):
                            store(t - 1, (u + 1) % HB)
                        if f == NF // 2 and not (is_last(b, B) and u == HB - 1):
                            wait_count(act, chunk_done, NF * t)
                            ffn.split_hi(act, t + 1, (u + 1) % HB)

            repeat(act, B, body)
            store(B * HB - 1, HB - 1)
            for u in range(HB):
                act.wait_ge(out_stored[u], 16 * B)

        @block.vector
        def _(dve):
            def split_chunk(n, f, count):
                slot = f % NW
                dve.wait_ge(w_loaded[slot], 32 * count)
                wait_count(dve, chunk_done, n - NW + 1)
                dve.tensor_copy(w_hi[:, slot, :, :], w_raw[:, slot, :, :]).then_inc(w_hi_ready, 1)
                dve.wait_ge(w_hi_ready, n + 1)
                dve.tensor_tensor(w_lo[:, slot, :, :], w_raw[:, slot, :, :], raw(w_hi[:, slot, :, :]), ALU.subtract
                                  ).then_inc(w_lo_ready, 1)

            split_chunk(0, 0, 1)
            split_chunk(1, 1, 1)

            def body(b):
                for u in range(HB):
                    t = HB * b + u
                    for f in range(NF):
                        n = NF * t + f
                        dve.wait_ge(h_hi_ready, n + 1)
                        dve.tensor_tensor(h_lo[:, f % 2, :], h_full[:, f % 2, :], raw(h_hi[:, f % 2, :]), ALU.subtract
                                          ).then_inc(h_lo_ready, 1)
                        if not (is_last(b, B) and u == HB - 1 and f >= NF - 2):
                            f2 = (f + 2) % NF
                            split_chunk(n + 2, f2, (NF // NW) * (t + (f + 2) // NF) + f2 // NW + 1)
                        if f == NF // 2 + 1 and not (is_last(b, B) and u == HB - 1):
                            ffn.split_lo(dve, t + 1, (u + 1) % HB)
                    dve.wait_ge(x1_biased, t + 1)
                    for j in range(TT):
                        if j < TT - 1:
                            dve.wait_ge(y_done, (TT - 1) * t + j + 1)
                        else:
                            dve.wait_ge(chunk_done, NF * (t + 1))
                        dve.scalar_tensor_tensor(x1[:, u, j, :], y_ps[:, j, :], gate_t[:, 0:1], x1[:, u, j, :],
                                                 ALU.mult, ALU.add).then_inc(res_ready, 1)

            dve.wait_ge(gate_ready, 1)
            repeat(dve, B, body)

        @block.tensor
        def _(pe):
            def hidden(t, b, u, f):
                n = NF * t + f
                if f == 0:
                    pe.wait_ge(z_lo_ready, t + 1)
                pe.wait_ge(w_lo_ready, n + 1)
                wait_count(pe, h_hi_ready, n - 1)
                for ct in range(CT):
                    cs = slice(ct * P, (ct + 1) * P)
                    for i, (w, l) in enumerate(((w_hi, 0), (w_hi, 1), (w_lo, 0))):
                        last = pe.matmul(h_ps[:, f % 2, :], w[:, f % NW, 0, cs], zT[:, u, l, ct, :],
                                         start=(ct == 0 and i == 0), stop=(ct == CT - 1 and i == 2))
                last.then_inc(hT_ready, 1)

            def result(t, f):
                n = NF * t + f
                pe.wait_ge(h_lo_ready, n + 1)
                for j in range(TT):
                    if f == 0:
                        wait_count(pe, res_ready, TT * (t - 1) + j + 1)
                    js = slice(j * P, (j + 1) * P)
                    for i, (a, w) in enumerate(((h_hi, w_hi), (h_hi, w_lo), (h_lo, w_hi))):
                        last = pe.matmul(y_ps[:, j, :], a[:, f % 2, js], w[:, f % NW, 1, :],
                                         start=(f == 0 and i == 0), stop=(f == NF - 1 and i == 2))
                    if f == NF - 1 and j < TT - 1:
                        last.then_inc(y_done, 1)
                last.then_inc(chunk_done, 1)

            hidden(0, 0, 0, 0)

            def body(b):
                for u in range(HB):
                    t = HB * b + u
                    for f in range(NF):
                        if f < NF - 1:
                            hidden(t, b, u, f + 1)
                        elif not (is_last(b, B) and u == HB - 1):
                            hidden(t + 1, b + (u + 1) // HB, (u + 1) % HB, 0)
                        result(t, f)

            repeat(pe, B, body)



def kernel(x, ctx_1024, g_xattn, g_ffn, L0_xattn_position_bias, L0_xattn_W_q, L0_xattn_W_kv, L0_xattn_W_proj,
           L0_ffn_Wr, L0_ffn_br, L0_ffn_W1, L0_ffn_b1, L0_ffn_W2, L0_ffn_b2):
    import numpy as np
    import concourse.bacc as bacc
    from concourse import mybir as mb
    from concourse.bass_utils import run_bass_kernel_spmd

    W1, b1 = np.asarray(L0_ffn_W1), np.asarray(L0_ffn_b1)
    E, D, F = W1.shape
    arrays = {
        "x": x,
        "ctxT": np.asarray(ctx_1024).transpose(0, 2, 1),
        "g_xattn": g_xattn,
        "g_ffn": g_ffn,
        "bias": L0_xattn_position_bias,
        "Wq": L0_xattn_W_q,
        "Wkv": L0_xattn_W_kv,
        "Wproj": L0_xattn_W_proj,
        "Wr": L0_ffn_Wr,
        "br": L0_ffn_br,
        "W1c": W1.reshape(E, D // 128, 128, F // 128, 128).transpose(0, 3, 2, 1, 4).reshape(E, F // 128, 128, D),
        "b1c": b1.reshape(E, F // 128, 128).transpose(0, 2, 1),
        "W2": L0_ffn_W2,
        "b2": L0_ffn_b2,
    }
    arrays = {k: np.ascontiguousarray(v) for k, v in arrays.items()}
    nc = bacc.Bacc("TRN2", target_bir_lowering=False, num_devices=1)
    ins = [nc.dram_tensor(k, v.shape, mb.dt.from_np(v.dtype), kind="ExternalInput").ap() for k, v in arrays.items()]
    shape = tuple(np.asarray(x).shape)
    out = nc.dram_tensor("out", (shape[0] * shape[1], shape[2]), mb.dt.float32, kind="ExternalOutput").ap()
    gated_block(nc, *ins, out)
    r = run_bass_kernel_spmd(nc, [arrays], core_ids=[0])
    return r.results[0]["out"].reshape(shape)
```
